# Optimizing a Trainium2 kernel written in Bass

```python
import numpy as np
import jax
import jax.numpy as jnp

def _softmax(x, axis=-1):
    return jax.nn.softmax(x, axis=axis)

def _gelu(x):
    return jax.nn.gelu(x, approximate=True)

def _silu(x):
    return jax.nn.silu(x)

def _sigmoid(x):
    return jax.nn.sigmoid(x)

def _layernorm(x, axis=-1, eps=1e-05):
    m = jnp.mean(x, axis=axis, keepdims=True)
    v = jnp.var(x, axis=axis, keepdims=True)
    return (x - m) / jnp.sqrt(v + eps)

def _scatter_add(tgt, idx, src, axis=0):
    return tgt.at[idx].add(src)

def _segment_sum(src, seg, n):
    return jax.ops.segment_sum(src, seg, n)
kernel_name = 'mk_xattn_seq_d2_seqx_r4_e066d5'

def setup_inputs(seed: int=0):
    np.random.seed(seed)
    _w = jnp.asarray

    def _rec_inputs():
        import jax
        import jax.numpy as jnp
        _rk = jax.random.key(seed)
        x = -0.0002928 + 1 * jax.random.normal(jax.random.fold_in(_rk, 1), (8, 256, 512), jnp.float32)
        _lenS = 256 - jax.random.randint(jax.random.fold_in(_rk, 7), (8,), 0, max(1, 256 // 4) + 1, jnp.int32)
        _lenS2 = 256 - jax.random.randint(jax.random.fold_in(_rk, 8), (8,), 0, max(1, 256 // 4) + 1, jnp.int32)
        _ctx_2048P = jax.random.normal(jax.random.fold_in(_rk, 11), (8, 16, 512), jnp.float32)
        _ctx_2048c = jax.random.dirichlet(jax.random.fold_in(_rk, 511), 0.3 * jnp.ones((16,), jnp.float32), (8, 256))
        _ctx_2048t = jnp.einsum('bsk,bkd->bsd', _ctx_2048c, _ctx_2048P)
        _ctx_2048t = _ctx_2048t * jax.lax.rsqrt(jnp.mean(jnp.square(_ctx_2048t)) + 1e-12) * 0.953939
        ctx_2048 = -1.39393e-06 + 0.999914 * (_ctx_2048t + 0.3 * jax.random.normal(jax.random.fold_in(_rk, 611), (8, 256, 512), jnp.float32))
        _validS = jnp.arange(256)[None, :] < _lenS[:, None]
        _validS2 = jnp.arange(256)[None, :] < _lenS2[:, None]
        _causal = jnp.tril(jnp.ones((256, 256), dtype=bool))
        mask_1x1xSxS2_fc1 = jnp.where(jnp.broadcast_to(_validS2[0:1, None, None, :], (1, 1, 256, 256)), 1.0, 0.0).astype(jnp.float32)
        mask_Bx1xSxS2_ff1 = jnp.where(jnp.ones((8, 1, 256, 256), dtype=bool), 1.0, 0.0).astype(jnp.float32)
        mask_Bx1xSxS2_ff0 = jnp.where(jnp.ones((8, 1, 256, 256), dtype=bool), 0.0, -1000000000.0).astype(jnp.float32)
        return (x, ctx_2048, mask_1x1xSxS2_fc1, mask_Bx1xSxS2_ff1, mask_Bx1xSxS2_ff0)
    x, ctx_2048, mask_1x1xSxS2_fc1, mask_Bx1xSxS2_ff1, mask_Bx1xSxS2_ff0 = _rec_inputs()

    def _L0_xattn_setup():
        import jax, jax.numpy as jnp
        import numpy as np
        H = 512
        NH = 16
        HD = H // NH
        EPS = 1e-05

        def gelu(x):
            return 0.5 * x * (1.0 + jnp.tanh(0.7978845608028654 * x * (1.0 + 0.044715 * x * x)))

        def layernorm(x, scale, bias):
            m = jnp.mean(x, axis=-1, keepdims=True)
            v = jnp.mean(jnp.square(x - m), axis=-1, keepdims=True)
            return (x - m) * jax.lax.rsqrt(v + EPS) * scale + bias

        def split_heads(x):
            b, s, _ = x.shape
            return x.reshape(b, s, NH, HD).transpose(0, 2, 1, 3)

        def merge_heads(x):
            b, nh, s, hd = x.shape
            return x.transpose(0, 2, 1, 3).reshape(b, s, nh * hd)

        def attention(q, k, v, mask):
            scores = jnp.einsum('bhqd,bhkd->bhqk', q, k) / jnp.sqrt(jnp.float32(HD))
            scores = scores * mask - 10000.0 * (1.0 - mask)
            probs = jax.nn.softmax(scores, axis=-1)
            return jnp.einsum('bhqk,bhkd->bhqd', probs, v)
        key = jax.random.key(seed)
        ks = jax.random.split(key, 16)
        b, s, t = (2, 256, 256)
        w = lambda k, i, o: jax.random.normal(k, (i, o), jnp.float32) * 0.02
        inp = {'hidden_states': jax.random.normal(ks[0], (b, s, H), jnp.float32), 'encoder_states': jax.random.normal(ks[1], (b, t, H), jnp.float32), 'ltor_mask': jnp.tril(jnp.ones((1, 1, s, s), jnp.float32)), 'cross_mask': jnp.ones((b, 1, s, t), jnp.float32), 'ln1_s': jnp.ones((H,), jnp.float32), 'ln1_b': jnp.zeros((H,), jnp.float32), 'w_qkv': w(ks[2], H, 3 * H), 'b_qkv': jnp.zeros((3 * H,), jnp.float32), 'w_ao': w(ks[3], H, H), 'b_ao': jnp.zeros((H,), jnp.float32), 'ln2_s': jnp.ones((H,), jnp.float32), 'ln2_b': jnp.zeros((H,), jnp.float32), 'w_q': w(ks[4], H, H), 'b_q': jnp.zeros((H,), jnp.float32), 'w_kv': w(ks[5], H, 2 * H), 'b_kv': jnp.zeros((2 * H,), jnp.float32), 'w_co': w(ks[6], H, H), 'b_co': jnp.zeros((H,), jnp.float32), 'ln3_s': jnp.ones((H,), jnp.float32), 'ln3_b': jnp.zeros((H,), jnp.float32), 'w1': w(ks[7], H, 4 * H), 'b1': jnp.zeros((4 * H,), jnp.float32), 'w2': w(ks[8], 4 * H, H), 'b2': jnp.zeros((H,), jnp.float32)}
        return inp
    _L0_xattn_all = _L0_xattn_setup()
    _L0_xattn_in = {k: v for k, v in _L0_xattn_all.items() if k in ('ln1_s', 'ln1_b', 'w_qkv', 'b_qkv', 'w_ao', 'b_ao', 'ln2_s', 'ln2_b', 'w_q', 'b_q', 'w_kv', 'b_kv', 'w_co', 'b_co', 'ln3_s', 'ln3_b', 'w1', 'b1', 'w2', 'b2')}
    del _L0_xattn_all

    def _L1_xattn_setup():
        import jax, jax.numpy as jnp
        import numpy as np
        H = 512
        NH = 32
        KVH = 8
        HD = H // NH
        GROUPS = NH // KVH
        EPS = 1e-06
        B, L, S = (4, 256, 256)

        def _gqa_forward(hidden_state, encoder_hidden_state, encoder_attention_mask, Wq, bq, Wk, bk, Wv, bv, Wo, bo, gamma, beta):
            b, l, _ = hidden_state.shape
            s = encoder_hidden_state.shape[1]
            q = hidden_state @ Wq + bq
            k = encoder_hidden_state @ Wk + bk
            v = encoder_hidden_state @ Wv + bv
            q = q.reshape(b, l, KVH, GROUPS, HD).transpose(0, 2, 3, 1, 4)
            k = k.reshape(b, s, KVH, HD).transpose(0, 2, 1, 3)
            v = v.reshape(b, s, KVH, HD).transpose(0, 2, 1, 3)
            scale = 1.0 / jnp.sqrt(jnp.asarray(HD, q.dtype))
            scores = jnp.einsum('bkgld,bksd->bkgls', q, k) * scale
            scores = scores + encoder_attention_mask[:, :, None, :, :]
            attn = jax.nn.softmax(scores, axis=-1)
            out = jnp.einsum('bkgls,bksd->bkgld', attn, v)
            out = out.transpose(0, 3, 1, 2, 4).reshape(b, l, H)
            out = out @ Wo + bo
            x = out + hidden_state
            mu = jnp.mean(x, axis=-1, keepdims=True)
            var = jnp.var(x, axis=-1, keepdims=True)
            return (x - mu) * jax.lax.rsqrt(var + EPS) * gamma + beta
        key = jax.random.key(seed)
        ks = jax.random.split(key, 12)
        sd = 0.02
        return {'hidden_state': jax.random.normal(ks[0], (B, L, H), jnp.float32), 'encoder_hidden_state': jax.random.normal(ks[1], (B, S, H), jnp.float32), 'encoder_attention_mask': jnp.zeros((B, 1, L, S), jnp.float32), 'Wq': jax.random.normal(ks[2], (H, H), jnp.float32) * sd, 'bq': jnp.zeros((H,), jnp.float32), 'Wk': jax.random.normal(ks[3], (H, KVH * HD), jnp.float32) * sd, 'bk': jnp.zeros((KVH * HD,), jnp.float32), 'Wv': jax.random.normal(ks[4], (H, KVH * HD), jnp.float32) * sd, 'bv': jnp.zeros((KVH * HD,), jnp.float32), 'Wo': jax.random.normal(ks[5], (H, H), jnp.float32) * sd, 'bo': jnp.zeros((H,), jnp.float32), 'gamma': jnp.ones((H,), jnp.float32), 'beta': jnp.zeros((H,), jnp.float32)}
    _L1_xattn_all = _L1_xattn_setup()
    _L1_xattn_in = {k: v for k, v in _L1_xattn_all.items() if k in ('Wq', 'bq', 'Wk', 'bk', 'Wv', 'bv', 'Wo', 'bo', 'gamma', 'beta')}
    del _L1_xattn_all
    return {'x': x, 'ctx_2048': ctx_2048, 'mask_1x1xSxS2_fc1': mask_1x1xSxS2_fc1, 'mask_Bx1xSxS2_ff1': mask_Bx1xSxS2_ff1, 'mask_Bx1xSxS2_ff0': mask_Bx1xSxS2_ff0, 'L0_xattn_ln1_s': _L0_xattn_in['ln1_s'], 'L0_xattn_ln1_b': _L0_xattn_in['ln1_b'], 'L0_xattn_w_qkv': _L0_xattn_in['w_qkv'], 'L0_xattn_b_qkv': _L0_xattn_in['b_qkv'], 'L0_xattn_w_ao': _L0_xattn_in['w_ao'], 'L0_xattn_b_ao': _L0_xattn_in['b_ao'], 'L0_xattn_ln2_s': _L0_xattn_in['ln2_s'], 'L0_xattn_ln2_b': _L0_xattn_in['ln2_b'], 'L0_xattn_w_q': _L0_xattn_in['w_q'], 'L0_xattn_b_q': _L0_xattn_in['b_q'], 'L0_xattn_w_kv': _L0_xattn_in['w_kv'], 'L0_xattn_b_kv': _L0_xattn_in['b_kv'], 'L0_xattn_w_co': _L0_xattn_in['w_co'], 'L0_xattn_b_co': _L0_xattn_in['b_co'], 'L0_xattn_ln3_s': _L0_xattn_in['ln3_s'], 'L0_xattn_ln3_b': _L0_xattn_in['ln3_b'], 'L0_xattn_w1': _L0_xattn_in['w1'], 'L0_xattn_b1': _L0_xattn_in['b1'], 'L0_xattn_w2': _L0_xattn_in['w2'], 'L0_xattn_b2': _L0_xattn_in['b2'], 'L1_xattn_Wq': _L1_xattn_in['Wq'], 'L1_xattn_bq': _L1_xattn_in['bq'], 'L1_xattn_Wk': _L1_xattn_in['Wk'], 'L1_xattn_bk': _L1_xattn_in['bk'], 'L1_xattn_Wv': _L1_xattn_in['Wv'], 'L1_xattn_bv': _L1_xattn_in['bv'], 'L1_xattn_Wo': _L1_xattn_in['Wo'], 'L1_xattn_bo': _L1_xattn_in['bo'], 'L1_xattn_gamma': _L1_xattn_in['gamma'], 'L1_xattn_beta': _L1_xattn_in['beta']}

def reference(x, ctx_2048, mask_1x1xSxS2_fc1, mask_Bx1xSxS2_ff1, mask_Bx1xSxS2_ff0, L0_xattn_ln1_s, L0_xattn_ln1_b, L0_xattn_w_qkv, L0_xattn_b_qkv, L0_xattn_w_ao, L0_xattn_b_ao, L0_xattn_ln2_s, L0_xattn_ln2_b, L0_xattn_w_q, L0_xattn_b_q, L0_xattn_w_kv, L0_xattn_b_kv, L0_xattn_w_co, L0_xattn_b_co, L0_xattn_ln3_s, L0_xattn_ln3_b, L0_xattn_w1, L0_xattn_b1, L0_xattn_w2, L0_xattn_b2, L1_xattn_Wq, L1_xattn_bq, L1_xattn_Wk, L1_xattn_bk, L1_xattn_Wv, L1_xattn_bv, L1_xattn_Wo, L1_xattn_bo, L1_xattn_gamma, L1_xattn_beta):
    import jax
    import jax.numpy as jnp

    def _L0_xattn_ref(hidden_states, encoder_states, ltor_mask, cross_mask, ln1_s, ln1_b, w_qkv, b_qkv, w_ao, b_ao, ln2_s, ln2_b, w_q, b_q, w_kv, b_kv, w_co, b_co, ln3_s, ln3_b, w1, b1, w2, b2):
        import jax, jax.numpy as jnp
        import numpy as np
        H = 512
        NH = 16
        HD = H // NH
        EPS = 1e-05

        def gelu(x):
            return 0.5 * x * (1.0 + jnp.tanh(0.7978845608028654 * x * (1.0 + 0.044715 * x * x)))

        def layernorm(x, scale, bias):
            m = jnp.mean(x, axis=-1, keepdims=True)
            v = jnp.mean(jnp.square(x - m), axis=-1, keepdims=True)
            return (x - m) * jax.lax.rsqrt(v + EPS) * scale + bias

        def split_heads(x):
            b, s, _ = x.shape
            return x.reshape(b, s, NH, HD).transpose(0, 2, 1, 3)

        def merge_heads(x):
            b, nh, s, hd = x.shape
            return x.transpose(0, 2, 1, 3).reshape(b, s, nh * hd)

        def attention(q, k, v, mask):
            scores = jnp.einsum('bhqd,bhkd->bhqk', q, k) / jnp.sqrt(jnp.float32(HD))
            scores = scores * mask - 10000.0 * (1.0 - mask)
            probs = jax.nn.softmax(scores, axis=-1)
            return jnp.einsum('bhqk,bhkd->bhqd', probs, v)
        ln_out = layernorm(hidden_states, ln1_s, ln1_b)
        qkv = ln_out @ w_qkv + b_qkv
        q, k, v = jnp.split(qkv, 3, axis=-1)
        ctx = merge_heads(attention(split_heads(q), split_heads(k), split_heads(v), ltor_mask))
        attn_out = ctx @ w_ao + b_ao
        x = hidden_states + attn_out
        ln_out = layernorm(x, ln2_s, ln2_b)
        q = ln_out @ w_q + b_q
        kv = encoder_states @ w_kv + b_kv
        k, v = jnp.split(kv, 2, axis=-1)
        ctx = merge_heads(attention(split_heads(q), split_heads(k), split_heads(v), cross_mask))
        cross_out = ctx @ w_co + b_co
        x = x + cross_out
        ln_out = layernorm(x, ln3_s, ln3_b)
        mlp_out = gelu(ln_out @ w1 + b1) @ w2 + b2
        return x + mlp_out

    def _L1_xattn_ref(hidden_state, encoder_hidden_state, encoder_attention_mask, Wq, bq, Wk, bk, Wv, bv, Wo, bo, gamma, beta):
        import jax, jax.numpy as jnp
        import numpy as np
        H = 512
        NH = 32
        KVH = 8
        HD = H // NH
        GROUPS = NH // KVH
        EPS = 1e-06
        B, L, S = (4, 256, 256)

        def _gqa_forward(hidden_state, encoder_hidden_state, encoder_attention_mask, Wq, bq, Wk, bk, Wv, bv, Wo, bo, gamma, beta):
            b, l, _ = hidden_state.shape
            s = encoder_hidden_state.shape[1]
            q = hidden_state @ Wq + bq
            k = encoder_hidden_state @ Wk + bk
            v = encoder_hidden_state @ Wv + bv
            q = q.reshape(b, l, KVH, GROUPS, HD).transpose(0, 2, 3, 1, 4)
            k = k.reshape(b, s, KVH, HD).transpose(0, 2, 1, 3)
            v = v.reshape(b, s, KVH, HD).transpose(0, 2, 1, 3)
            scale = 1.0 / jnp.sqrt(jnp.asarray(HD, q.dtype))
            scores = jnp.einsum('bkgld,bksd->bkgls', q, k) * scale
            scores = scores + encoder_attention_mask[:, :, None, :, :]
            attn = jax.nn.softmax(scores, axis=-1)
            out = jnp.einsum('bkgls,bksd->bkgld', attn, v)
            out = out.transpose(0, 3, 1, 2, 4).reshape(b, l, H)
            out = out @ Wo + bo
            x = out + hidden_state
            mu = jnp.mean(x, axis=-1, keepdims=True)
            var = jnp.var(x, axis=-1, keepdims=True)
            return (x - mu) * jax.lax.rsqrt(var + EPS) * gamma + beta
        return _gqa_forward(hidden_state, encoder_hidden_state, encoder_attention_mask, Wq, bq, Wk, bk, Wv, bv, Wo, bo, gamma, beta)
    x = _L0_xattn_ref(x, ctx_2048, mask_1x1xSxS2_fc1, mask_Bx1xSxS2_ff1, L0_xattn_ln1_s, L0_xattn_ln1_b, L0_xattn_w_qkv, L0_xattn_b_qkv, L0_xattn_w_ao, L0_xattn_b_ao, L0_xattn_ln2_s, L0_xattn_ln2_b, L0_xattn_w_q, L0_xattn_b_q, L0_xattn_w_kv, L0_xattn_b_kv, L0_xattn_w_co, L0_xattn_b_co, L0_xattn_ln3_s, L0_xattn_ln3_b, L0_xattn_w1, L0_xattn_b1, L0_xattn_w2, L0_xattn_b2)
    x = _L1_xattn_ref(x, ctx_2048, mask_Bx1xSxS2_ff0, L1_xattn_Wq, L1_xattn_bq, L1_xattn_Wk, L1_xattn_bk, L1_xattn_Wv, L1_xattn_bv, L1_xattn_Wo, L1_xattn_bo, L1_xattn_gamma, L1_xattn_beta)
    return x

_drawn_inputs = setup_inputs


def setup_inputs(seed=0):
    import zlib

    import numpy as np

    out = dict(_drawn_inputs(seed))
    spreads = {'L0_xattn_ln1_s': (1.0, 0.6),
     'L0_xattn_ln1_b': (0.0, 0.4),
     'L0_xattn_b_qkv': (0.0, 0.1),
     'L0_xattn_b_ao': (0.0, 0.1),
     'L0_xattn_ln2_s': (1.0, 0.6),
     'L0_xattn_ln2_b': (0.0, 0.8),
     'L0_xattn_b_q': (0.0, 2.0),
     'L0_xattn_b_kv': (0.0, 0.1),
     'L0_xattn_b_co': (0.0, 0.1),
     'L0_xattn_ln3_s': (1.0, 0.2),
     'L0_xattn_ln3_b': (0.0, 0.327),
     'L0_xattn_b1': (0.0, 0.1),
     'L0_xattn_b2': (0.0, 0.1),
     'L1_xattn_bq': (0.0, 0.8),
     'L1_xattn_bk': (0.0, 2.0),
     'L1_xattn_bv': (0.0, 0.1),
     'L1_xattn_bo': (0.0, 0.1),
     'L1_xattn_gamma': (1.0, 0.2),
     'L1_xattn_beta': (0.0, 0.1)}
    factors = {'L0_xattn_w_q': 7.436, 'L1_xattn_Wq': 7.532, 'L1_xattn_Wk': 7.344}
    for name, (base, spread) in spreads.items():
        noise = np.random.default_rng([zlib.crc32(name.encode()), seed]).standard_normal(out[name].shape)
        drawn = base * np.exp(spread * noise) if base else spread * noise
        out[name] = jnp.asarray(drawn.astype(out[name].dtype))
    for name, factor in factors.items():
        out[name] = (out[name] * factor).astype(out[name].dtype)
    return out
```

```python
from collections import namedtuple
from contextlib import ExitStack, contextmanager

import concourse.bass as bass
import numpy as np
from concourse import mybir

F32 = mybir.dt.float32
F32R = mybir.dt.float32r
ALU = mybir.AluOpType
ACT = mybir.ActivationFunctionType

P = 128
BATCHES, TOKENS, D = 8, 256, 512
TOK = TOKENS // P
KT = D // P
TILES = BATCHES * TOK
GROUPS = D // P
QUAD = 4
PROBS = 4
STAGED = 4
BIG = 3.0e38
GELU_C, GELU_A = 0.7978845608028654, 0.044715


def at(batch, per, extra=0):
    r, k = batch
    return r * (2 * per) + (k * per + extra)


def wait(eng, sem, value):
    if not isinstance(value, int) or value > 0:
        eng.wait_ge(sem, value)


def passed(eng, sem, value, count):
    wait(eng, sem, value)
    if not isinstance(value, int):
        eng.sem_inc(count, 1)


def nxt(batch):
    return batch[0], batch[1] + 1


def prv(batch):
    return batch[0], batch[1] - 1


def over_batches(eng, step):
    step((0, -1), False, True, False)
    step((0, 0), True, True, False)
    with eng.Fori(0, (BATCHES - 2) // 2) as r:
        step((r, 1), True, True, True)
        step((r, 2), True, True, True)
    step((BATCHES // 2 - 1, 1), True, False, True)
    step((BATCHES // 2, 0), False, False, True)


def semaphores(nc, ctx, stage, names, **sets):
    sems = {name: ctx.enter_context(nc.semaphore(f"{stage}_{name}")) for name in names.split()}
    return namedtuple("Signals", [*sems, *sets])(**sems, **sets)


def passes(nc, out, stationary, moving, first, last):
    (sh, sl), (mh, ml) = stationary, moving
    nc.tensor.matmul(out, sh, mh, start=first, stop=False)
    nc.tensor.matmul(out, sh, ml, start=False, stop=False)
    return nc.tensor.matmul(out, sl, mh, start=False, stop=last)



def chunks_of(w, high, low, rows, at_col, scale=None):
    n = w.shape[1]
    for k in range(rows // P):
        for c in range(0, n, 512):
            m = min(512, n - c)
            yield (w[k * P:(k + 1) * P, c:c + m], high[:, k, at_col + c:at_col + c + m],
                   low[:, k, at_col + c:at_col + c + m], scale)


def load_chunks(sp, chunks, ring, s):
    for n, (src, _, _, _) in enumerate(chunks):
        wait(sp, s.w_split, n - STAGED + 1)
        sp.dma_start(ring[:, n % STAGED, 0:src.shape[1]], src).then_inc(s.w_in[n % STAGED], 16)


def high_chunks(nc, act, chunks, ring, s):
    for n, (src, high, _, scale) in enumerate(chunks):
        act.wait_ge(s.w_in[n % STAGED], 16 * (n // STAGED + 1))
        nc.scalar.activation(high, ring[:, n % STAGED, 0:src.shape[1]], ACT.Copy,
                             scale=1.0 if scale is None else scale).then_inc(s.w_high, 1)


def low_chunks(nc, dve, chunks, ring, s):
    for n, (src, high, low, scale) in enumerate(chunks):
        dve.wait_ge(s.w_high, n + 1)
        nc.vector.scalar_tensor_tensor(out=low, in0=ring[:, n % STAGED, 0:src.shape[1]],
                                       scalar=1.0 if scale is None else scale, in1=high.bitcast(F32),
                                       op0=ALU.mult, op1=ALU.subtract).then_inc(s.w_split, 1)


def row_of(vector, n):
    return vector.rearrange("(a n) -> a n", a=1).broadcast_to([P, n])


def attention_stage(nc, ctx, name, shared, out, *, q_src, weights, biases, norm, mask, mask_kind,
                    enc, heads, kv_heads, first_stage=False):
    x, mean, rstd, stats, ident, banks = (shared[n] for n in ("x", "mean", "rstd", "stats", "ident", "banks"))
    HD = D // heads
    KVD = kv_heads * HD
    REP = heads // kv_heads
    K = 3 * HD
    NU = heads
    NQ = NU // QUAD
    PER_GROUP = P // HD
    QPG = PER_GROUP // QUAD
    QS = -1.0 / float(np.sqrt(HD))
    multiply = mask_kind != "added"
    mask_bufs = 1 if mask_kind == "shared" else 2
    small = HD < 32
    LAG = 3

    def sb(n, shape, dt=F32):
        return ctx.enter_context(nc.sbuf_tensor(f"{name}_{n}", shape, dt))

    q_w, k_w, v_w, o_w = weights
    q_b, k_b, v_b, o_b = biases
    KB = KVD // P
    cols = {"q": 0, "k": D, "v": D + KVD, "o": D + 2 * KVD}
    NC = 2 * D + 2 * KVD
    w_hi, w_lo = sb("w_hi", [P, KT, NC], F32R), sb("w_lo", [P, KT, NC], F32R)
    xn = sb("xn", [P, TOK, D])
    enc_in = sb("enc_in", [P, D]) if enc is not None else None
    xt_hi, xt_lo = sb("xt_hi", [P, KT, TOKENS], F32R), sb("xt_lo", [P, KT, TOKENS], F32R)
    part_hi, part_lo = sb("part_hi", [P, 2, 2, TOKENS], F32R), sb("part_lo", [P, 2, 2, TOKENS], F32R)
    q_stack = sb("q_stack", [K, heads, TOKENS], F32R)
    k_bufs = 2 if small else 1
    k_stack = sb("k_stack", [K, k_bufs, kv_heads, TOKENS], F32R)
    value = sb("value", [P, 2, TOK, kv_heads, 3 * HD]) if small else sb("value", [P, 2, TOK, D])
    masks = sb("masks", [P, mask_bufs, TOK, TOKENS])
    offset = sb("offset", [P, mask_bufs, TOK, TOKENS]) if multiply else masks
    prob = sb("prob", [P, PROBS, TOK, TOKENS])
    ring = prob[:, :, :, :].rearrange("p s t n -> p s (t n)")
    neg_max, sums, inv = (sb(n, [P, PROBS, TOK]) for n in ("neg_max", "sums", "inv"))
    prob_t = sb("prob_t", [P, 2 * QUAD, TOK, TOKENS])
    ctx_hi, ctx_lo = sb("ctx_hi", [P, GROUPS, TOKENS], F32R), sb("ctx_lo", [P, GROUPS, TOKENS], F32R)
    q_bias, k_bias = sb("q_bias", [P, GROUPS]), sb("k_bias", [P, KB])
    v_bias, o_bias = sb("v_bias", [P, KVD]), sb("o_bias", [P, D])
    if norm:
        n_scale, n_bias = sb("n_scale", [P, D]), sb("n_bias", [P, D])

    score_bank, pt_bank = banks[0:2], banks[2:4]
    ctx_bank, proj_bank = [banks[4], banks[7]], banks[5:7]

    w_in = [ctx.enter_context(nc.semaphore(f"{name}_w_in{i}")) for i in range(STAGED)]
    stacked = {}
    s = semaphores(nc, ctx, name, """
        const_in w_high w_split x_in neg_bias value_zero stats_in std_in rstd_in
        normed scaled affine enc_loaded mask_loaded offset_in
        proj_done high_done proj_free scores_done masked maxed exp_done inv_done prob_done
        turned pt_even pt_odd pv_done ctx_high ctx_split out_done x_biased out_added stats_done
        sp_passed pool_passed dve_passed""", w_in=w_in, stacked=stacked)

    uses = []
    if enc is not None:
        uses += [("turn_enc", 0), ("turn_enc", 1)]
    else:
        uses += [("turn_x", 0), ("turn_x", 1)]
    uses += [("v", 0)] if small else [("v", 0), ("v", 1)]
    uses += [("k", 0)] if small else [("k", 0), ("k", 1)]
    if enc is not None:
        uses += [("turn_x", 0), ("turn_x", 1)]
    uses += [("q", 0), ("q", 1)]
    NP = len(uses)
    assert NP % 2 == 0
    index = {u: j for j, u in enumerate(uses)}
    highs = [u for u in uses if u[0] != "v"]
    NH = len(highs)
    parts = [u for u in uses if u[0] in "qk"]
    stacked.update({u: ctx.enter_context(nc.semaphore(f"{name}_stacked_{u[0]}{u[1]}")) for u in parts})
    blocks = {u: min(2, KB) if u[0] == "k" else 2 for u in parts}
    n_dma = {u: 3 * PER_GROUP for u in parts}

    gap = (NU - 3) / (NP + 1)
    slot_of = {j: int(3 + (j + 1) * gap) for j in range(NP)}
    slot_of[NP - 1] = NU + 1
    SLOTS = NU + LAG + 3

    def uses_at(t):
        return [j for j in range(NP) if slot_of[j] == t]

    def head_of(u):
        if not small:
            return u
        g, r = divmod(u, PER_GROUP)
        return g * PER_GROUP + 2 * (r % QUAD) + r // QUAD

    def units_before(u):
        kind, pair = u
        return 0 if kind == "k" and small else (pair + 1) * 2 * PER_GROUP

    chunks = []
    for key, w, sc in (("v", v_w, None), ("k", k_w, None), ("q", q_w, QS), ("o", o_w, None)):
        chunks += list(chunks_of(w, w_hi, w_lo, D, cols[key], sc))

    def w_part(key, k, a, b):
        c = cols[key]
        return w_hi[:, k, c + a:c + b], w_lo[:, k, c + a:c + b]

    block = ctx.enter_context(nc.Block())

    @block.sync
    def _(sp):
        small_in = [(q_bias[:, :], q_b.rearrange("(j p) -> p j", p=P)),
                    (k_bias[:, :], k_b.rearrange("(j p) -> p j", p=P)),
                    (v_bias[:, :], row_of(v_b, KVD)), (o_bias[:, :], row_of(o_b, D))]
        if norm:
            small_in += [(n_scale[:, :], row_of(norm[0], D)), (n_bias[:, :], row_of(norm[1], D))]
        if first_stage:
            for b in range(BATCHES):
                sp.dma_start(x[:, TOK * b:TOK * (b + 1), :],
                             shared["x_dram"][b].rearrange("(t p) d -> p t d", p=P)).then_inc(s.x_in, 16)
        for dst, src in small_in:
            sp.dma_start(dst, src, allow_slow_non_contiguous=True).then_inc(s.const_in, 16)
        load_chunks(sp, chunks, ring, s)

        def load_enc(b, t):
            rows = enc.rearrange("b (t p) d -> (b t) p d", p=P)
            n = at(b, TOK, t)
            src = rows[n] if isinstance(n, int) else rows[bass.ds(n, 1)].rearrange("a p d -> (a p) d")
            sp.dma_start(enc_in[:, :], src).then_inc(s.enc_loaded, 16)

        def load_mask(b):
            n = at(b, 1)
            src = mask[0:1] if mask_kind == "shared" else mask[bass.ds(n, 1)] if not isinstance(n, int) else mask[n:n + 1]
            sp.dma_start(masks[:, b[1] % mask_bufs, :, :],
                         src.rearrange("a b (t p) n -> p (a b t) n", p=P)).then_inc(s.mask_loaded, 16)

        def stack(u, p):
            j, slot = index[u], parts.index(u) % 2
            passed(sp, s.proj_free, at(p, NP, j + 1), s.sp_passed)
            before = units_before(u)
            passed(sp, s.scores_done, at(prv(p), NU, before), s.sp_passed)
            for r in range(PER_GROUP):
                for part in range(3):
                    low = part == (1 if u[0] == "q" else 2)
                    src = (part_lo if low else part_hi)[r * HD:(r + 1) * HD, slot, 0:blocks[u], :]
                    if u[0] == "q" or not small:
                        dst = q_stack if u[0] == "q" else k_stack[:, 0]
                        h = 2 * PER_GROUP * u[1] + r
                        dst = dst[part * HD:(part + 1) * HD, h:h + PER_GROUP * (blocks[u] - 1) + 1:PER_GROUP, :]
                    else:
                        dst = k_stack[part * HD:(part + 1) * HD, p[1] % 2, r:r + 1, :]
                    sp.dma_start(dst.bitcast(F32), src.bitcast(F32)).then_inc(s.stacked[u], 16)

        def step(b, attend, project, finish):
            if not project:
                return
            p = nxt(b)
            order = parts if small else [("k", 0), ("q", 0), ("k", 1), ("q", 1)]
            if enc is not None:
                passed(sp, s.proj_done, at(prv(p), NP, index[("turn_enc", 1)] + 1), s.sp_passed)
                load_enc(p, 0)
            if mask_kind != "shared" or not attend:
                if attend:
                    passed(sp, s.maxed, at(b, NU, 0), s.sp_passed)
                load_mask(p)
            if enc is not None:
                passed(sp, s.proj_done, at(p, NP, index[("turn_enc", 0)] + 1), s.sp_passed)
                load_enc(p, 1)
            for u in order:
                stack(u, p)

        over_batches(sp, step)

    @block.gpsimd
    def _(pool):
        if first_stage:
            nc.gpsimd.memset(ident[:, :], 0.0).then_inc(shared["ident_in"], 1)
            pool.wait_ge(shared["ident_in"], 1)
            nc.gpsimd.affine_select(out=ident[:, :], in_=ident[:, :], compare_op=ALU.not_equal, fill=1.0,
                                    base=0, pattern=[[-1, P]], channel_multiplier=1).then_inc(shared["ident_in"], 1)
        if small:
            nc.gpsimd.memset(value[:, :, :, :, :], 0.0).then_inc(s.value_zero, 1)
        pool.wait_ge(s.const_in, 16 * (6 if norm else 4))
        nc.gpsimd.tensor_scalar(q_bias[:, :], q_bias[:, :], QS, None, ALU.mult).then_inc(s.neg_bias, 1)

        def affine(p):
            if not norm:
                return
            for t in range(TOK):
                pool.wait_ge(s.normed, at(p, TOK, t + 1))
                nc.gpsimd.tensor_tensor(xn[:, t, :], xn[:, t, :], n_scale[:, :], ALU.mult).then_inc(s.scaled, 1)
            for t in range(TOK):
                pool.wait_ge(s.scaled, at(p, TOK, t + 1))
                nc.gpsimd.tensor_tensor(xn[:, t, :], xn[:, t, :], n_bias[:, :], ALU.add).then_inc(s.affine, 1)

        def offsets(p):
            buf = p[1] % mask_bufs
            pool.wait_ge(s.mask_loaded, at(p, 16, 16) if mask_kind != "shared" else 16)
            pool.sem_inc(s.pool_passed, 1)
            a, c = (1.0, -10000.0) if multiply else (0.0, -1.0)
            nc.gpsimd.tensor_scalar(offset[:, buf, :, :], masks[:, buf, :, :], a, c, ALU.subtract,
                                    ALU.mult).then_inc(s.offset_in, 1)

        def bias_x(b):
            wait(pool, s.normed, at(b, TOK, TOK))
            for t in range(TOK):
                tile = x[:, bass.ds(at(b, TOK, t), 1), :] if not isinstance(at(b, 1), int) else x[:, at(b, TOK, t):at(b, TOK, t) + 1, :]
                nc.gpsimd.tensor_tensor(tile, tile, o_bias[:, :].rearrange("p (a d) -> p a d", a=1),
                                        ALU.add).then_inc(s.x_biased, 1)

        def step(b, attend, project, finish):
            p = nxt(b)
            if not attend:
                if project:
                    offsets(p)
                    affine(p)
                return
            for t in range(SLOTS):
                if 1 <= t <= NU:
                    u = t - 1
                    pool.wait_ge(s.inv_done, at(b, NU, u + 1))
                    pr = prob[:, u % PROBS, :, :]
                    nc.gpsimd.tensor_tensor(pr, pr, inv[:, u % PROBS, :].rearrange("p (t a) -> p t a", a=1)
                                            .broadcast_to([P, TOK, TOKENS]), ALU.mult).then_inc(s.prob_done, 1)
                if t == 1 and project:
                    affine(p)
                if t == 4 and project and mask_kind != "shared":
                    offsets(p)
                if t == 6:
                    bias_x(b)

        over_batches(pool, step)

    @block.scalar
    def _(act):
        high_chunks(nc, act, chunks, ring, s)
        if norm:
            act.wait_ge(s.stats_in, 1)
            nc.scalar.activation(rstd[:, :], rstd[:, :], ACT.Sqrt).then_inc(s.std_in, 1)
        act.wait_ge(s.neg_bias, 1)

        def high(j, p):
            u = uses[j]
            bank = proj_bank[j % 2]
            act.wait_ge(s.proj_done, at(p, NP, j + 1))
            if u[0] in ("turn_x", "turn_enc"):
                nc.scalar.activation(xt_hi[:, :, u[1] * P:(u[1] + 1) * P], bank[:, :].rearrange("p (k t) -> p k t", k=KT),
                                     ACT.Copy).then_inc(s.high_done, 1)
                return
            i = parts.index(u)
            slot = i % 2
            if i >= 2:
                v = parts[i - 2]
                wait(act, s.stacked[v], at(p, 16 * n_dma[v], 16 * n_dma[v]))
            else:
                v = parts[len(parts) - 2 + i] if len(parts) % 2 == 0 else None
                if v is None:
                    for v in parts:
                        wait(act, s.stacked[v], at(prv(p), 16 * n_dma[v], 16 * n_dma[v]))
                else:
                    wait(act, s.stacked[v], at(prv(p), 16 * n_dma[v], 16 * n_dma[v]))
            bias = q_bias if u[0] == "q" else k_bias
            for m in range(blocks[u]):
                ins = nc.scalar.activation(part_hi[:, slot, m, :], bank[:, m * TOKENS:(m + 1) * TOKENS], ACT.Identity,
                                           bias=bias[:, 2 * u[1] + m:2 * u[1] + m + 1])
            ins.then_inc(s.high_done, 1)

        def evacuate(u, b):
            act.wait_ge(s.turned, at(b, NU, u + 1))
            if u % QUAD < 2:
                wait(act, s.pv_done, at(b, NQ, u // QUAD - 1))
            nc.scalar.activation(prob_t[:, u % (2 * QUAD), :, :].rearrange("p t n -> p (t n)"), pt_bank[u % 2][:, :],
                                 ACT.Copy).then_inc(s.pt_odd if u % 2 else s.pt_even, 1)

        def step(b, attend, project, finish):
            p = nxt(b)
            if not attend:
                if project:
                    for j in range(NP):
                        if uses[j] in highs:
                            high(j, p)
                return
            for t in range(SLOTS + 1):
                if project:
                    for j in uses_at(t - 1):
                        if uses[j] in highs:
                            high(j, p)
                u = t - LAG
                if 0 <= u < NU and (not small or u % 2 == 0):
                    evacuate(u, b)
                if t < NU:
                    act.wait_ge(s.maxed, at(b, NU, t + 1))
                    for h in range(TOK):
                        pr = prob[:, t % PROBS, h, :]
                        ins = nc.scalar.activation(pr, pr, ACT.Exp, bias=neg_max[:, t % PROBS, h:h + 1], scale=-1.0,
                                                   accum_out=sums[:, t % PROBS, h:h + 1])
                    ins.then_inc(s.exp_done, 1)
                q = (t - 8) // QUAD if t >= 8 and (t - 8) % QUAD == 0 else None
                if q is not None and q < NQ and (q + 1) % QPG == 0:
                    g = q // QPG
                    act.wait_ge(s.pv_done, at(b, NQ, q + 1))
                    wait(act, s.out_done, at(b, TOK))
                    nc.scalar.activation(ctx_hi[:, g, :], ctx_bank[g % 2][:, 0:TOKENS], ACT.Copy).then_inc(s.ctx_high, 1)

        over_batches(act, step)

    @block.tensor
    def _(pe):
        pe.wait_ge(s.w_split, len(chunks))
        if first_stage:
            pe.wait_ge(shared["ident_in"], 2)

        def project_use(j, p):
            u = uses[j]
            bank = proj_bank[j % 2]
            wait(pe, s.proj_free, at(p, NP, j - 1))
            if j < 2:
                wait(pe, s.out_added, at(prv(p), TOK, j + 1 - TOK))
            if u[0] in ("turn_x", "turn_enc"):
                t = u[1]
                if u[0] == "turn_x":
                    pe.wait_ge(s.affine if norm else s.normed, at(p, TOK, t + 1))
                    src = xn[:, t, :]
                else:
                    pe.wait_ge(s.enc_loaded, at(p, 16 * TOK, 16 * (t + 1)))
                    src = enc_in[:, :]
                for k in range(KT):
                    ins = nc.tensor.transpose(bank[:, k * P:(k + 1) * P], src[:, k * P:(k + 1) * P], ident[:, :])
            elif u[0] == "v":
                pe.wait_ge(s.proj_free, at(p, NP, j if small or u[1] == 0 else j - 1))
                for t in (range(TOK) if small else [u[1]]):
                    for k in range(KT):
                        rows = xt_hi[:, k, t * P:(t + 1) * P], xt_lo[:, k, t * P:(t + 1) * P]
                        c = t * KVD if small else 0
                        ins = passes(nc, bank[:, c:c + KVD], rows, w_part("v", k, 0, KVD), k == 0, k == KT - 1)
            else:
                if u[0] == "q" and u[1] == 0:
                    pe.wait_ge(s.proj_free, at(p, NP, index[("turn_x", 1)] + 1))
                for m in range(blocks[u]):
                    c = (2 * u[1] + m) * P
                    for k in range(KT):
                        ins = passes(nc, bank[:, m * TOKENS:(m + 1) * TOKENS], w_part(u[0], k, c, c + P),
                                     (xt_hi[:, k, :], xt_lo[:, k, :]), k == 0, k == KT - 1)
            ins.then_inc(s.proj_done, 1)

        def scores(u, b):
            h = head_of(u)
            wait(pe, s.masked if multiply else s.maxed, at(b, NU, u - 1))
            if u % (2 * PER_GROUP) == 0:
                pair = u // (2 * PER_GROUP)
                v = ("q", pair)
                pe.wait_ge(s.stacked[v], at(b, 16 * n_dma[v], 16 * n_dma[v]))
                v = ("k", 0 if small else pair)
                pe.wait_ge(s.stacked[v], at(b, 16 * n_dma[v], 16 * n_dma[v]))
            for t in range(TOK):
                ins = nc.tensor.matmul(score_bank[u % 2][:, t * TOKENS:(t + 1) * TOKENS], q_stack[:, h, t * P:(t + 1) * P],
                                       k_stack[:, b[1] % k_bufs, h // REP, :], start=True, stop=True)
            ins.then_inc(s.scores_done, 1)

        def turn(u, b):
            pe.wait_ge(s.prob_done, at(b, NU, u + 1))
            wait(pe, s.pt_odd if u % 2 else s.pt_even, at(b, NU // 2, u // 2))
            for kt in range(TOK):
                for t in range(TOK):
                    c = kt * TOKENS + t * P
                    ins = nc.tensor.transpose(pt_bank[u % 2][:, c:c + P], prob[:, u % PROBS, t, kt * P:(kt + 1) * P], ident[:, :])
            ins.then_inc(s.turned, 1)

        def times_values(q, b):
            g = q // QPG
            pe.wait_ge(s.pt_even, at(b, NU // 2, 2 * (q + 1)))
            pe.wait_ge(s.pt_odd, at(b, NU // 2, 2 * (q + 1)))
            if q == 0:
                last_v = max(index[u] for u in uses if u[0] == "v")
                pe.wait_ge(s.proj_free, at(b, NP, last_v + 1))
            if q % QPG == 0:
                wait(pe, s.ctx_split, at(b, GROUPS, g - 1))
            first, last = q % QPG == 0, q % QPG == QPG - 1
            for kt in range(TOK):
                for i in range(QUAD):
                    u = q * QUAD + i
                    h = head_of(u)
                    if small:
                        c = HD * (1 - q % 2)
                        v = value[:, b[1] % 2, kt, h // REP, c:c + 2 * HD]
                    else:
                        v = value[:, b[1] % 2, kt, h * HD:(h + 1) * HD]
                    ins = nc.tensor.matmul(ctx_bank[g % 2][32 * i:32 * i + 32, 0:TOKENS], v, prob_t[:, u % (2 * QUAD), kt, :],
                                           start=first and kt == 0, stop=last and kt == TOK - 1)
            ins.then_inc(s.pv_done, 1)

        def project_out(t, b, last_projected, projected_between):
            if t == 0:
                pe.wait_ge(s.ctx_split, at(b, GROUPS, GROUPS))
            wait(pe, s.proj_free, at(last_projected, NP, NP + t - 1))
            if not projected_between:
                wait(pe, s.out_added, at(b, TOK, t + 1 - TOK))
            for k in range(KT):
                rows = ctx_hi[:, k, t * P:(t + 1) * P], ctx_lo[:, k, t * P:(t + 1) * P]
                ins = passes(nc, proj_bank[t][:, :], rows, w_part("o", k, 0, D), k == 0, k == KT - 1)
            ins.then_inc(s.out_done, 1)

        def step(b, attend, project, finish):
            p = nxt(b)
            if not attend:
                if project:
                    for j in range(NP):
                        project_use(j, p)
                if finish:
                    for t in range(TOK):
                        project_out(t, prv(b), prv(b), False)
                return
            for t in range(SLOTS):
                if t < NU:
                    scores(t, b)
                if 0 <= t - LAG < NU:
                    turn(t - LAG, b)
                if t >= 7 and (t - 7) % QUAD == 0 and (t - 7) // QUAD < NQ:
                    times_values((t - 7) // QUAD, b)
                if finish and t in (1, 2):
                    project_out(t - 1, prv(b), b, True)
                if project:
                    for j in uses_at(t):
                        project_use(j, p)

        over_batches(pe, step)

    @block.vector
    def _(dve):
        if norm:
            if first_stage:
                for i in range(TILES):
                    if i % TOK == 0:
                        dve.wait_ge(s.x_in, 16 * BATCHES)
                    nc.vector.bn_stats(stats[:, i, :], x[:, i, :]).then_inc(s.stats_done, 1)
                dve.wait_ge(s.stats_done, TILES)
            aggregate(nc, shared, 1e-5).then_inc(s.stats_in, 1)
        low_chunks(nc, dve, chunks, ring, s)
        if norm:
            dve.wait_ge(s.std_in, 1)
            nc.vector.reciprocal(rstd[:, :], rstd[:, :]).then_inc(s.rstd_in, 1)
            dve.wait_ge(s.rstd_in, 1)
        dve.wait_ge(s.const_in, 16 * (6 if norm else 4))
        dve.wait_ge(s.neg_bias, 1)
        if small:
            dve.wait_ge(s.value_zero, 1)

        def tile_of(arr, n):
            return arr[:, n:n + 1] if isinstance(n, int) else arr[:, bass.ds(n, 1)]

        def normalise(t, p):
            wait(dve, s.proj_done, at(prv(p), NP, index[("turn_x", 1)] + 1))
            n = at(p, TOK, t)
            src = x[:, n:n + 1, :] if isinstance(n, int) else x[:, bass.ds(n, 1), :]
            dst = xn[:, t:t + 1, :]
            if norm:
                ins = nc.vector.tensor_scalar(dst, src, tile_of(mean, n), tile_of(rstd, n), ALU.subtract, ALU.mult)
            else:
                ins = nc.vector.tensor_copy(dst, src)
            ins.then_inc(s.normed, 1)

        def low(j, p):
            u = uses[j]
            bank = proj_bank[j % 2]
            if u[0] == "v":
                dve.wait_ge(s.proj_done, at(p, NP, j + 1))
                if small:
                    for t in range(TOK):
                        ins = nc.vector.tensor_tensor(value[:, p[1] % 2, t, :, HD:2 * HD],
                                                      bank[:, t * KVD:(t + 1) * KVD].rearrange("p (h d) -> p h d", d=HD),
                                                      v_bias[:, :].rearrange("p (h d) -> p h d", d=HD), ALU.add)
                else:
                    ins = nc.vector.tensor_tensor(value[:, p[1] % 2, u[1], :], bank[:, :], v_bias[:, :], ALU.add)
                ins.then_inc(s.proj_free, 1)
                return
            dve.wait_ge(s.high_done, at(p, NH, highs.index(u) + 1))
            if u[0] in ("turn_x", "turn_enc"):
                c = slice(u[1] * P, (u[1] + 1) * P)
                nc.vector.tensor_tensor(xt_lo[:, :, c], bank[:, :].rearrange("p (k t) -> p k t", k=KT),
                                        xt_hi[:, :, c].bitcast(F32), ALU.subtract).then_inc(s.proj_free, 1)
                return
            slot = parts.index(u) % 2
            bias = q_bias if u[0] == "q" else k_bias
            for m in range(blocks[u]):
                ins = nc.vector.scalar_tensor_tensor(out=part_lo[:, slot, m, :], in0=bank[:, m * TOKENS:(m + 1) * TOKENS],
                                                     scalar=bias[:, 2 * u[1] + m:2 * u[1] + m + 1],
                                                     in1=part_hi[:, slot, m, :].bitcast(F32), op0=ALU.add, op1=ALU.subtract)
            ins.then_inc(s.proj_free, 1)

        def add_out(t, b):
            dve.wait_ge(s.out_done, at(b, TOK, t + 1))
            dve.wait_ge(s.x_biased, at(b, TOK, t + 1))
            n = at(b, TOK, t)
            tile = x[:, n:n + 1, :] if isinstance(n, int) else x[:, bass.ds(n, 1), :]
            nc.vector.tensor_tensor(tile, proj_bank[t][:, :].rearrange("p (a d) -> p a d", a=1), tile,
                                    ALU.add).then_inc(s.out_added, 1)

        def take_stats(t, b):
            dve.wait_ge(s.out_added, at(b, TOK, t + 1))
            n = at(b, TOK, t)
            tile = x[:, n, :] if isinstance(n, int) else x[:, bass.ds(n, 1), :]
            st = stats[:, n, :] if isinstance(n, int) else stats[:, bass.ds(n, 1), :]
            nc.vector.bn_stats(st, tile).then_inc(s.stats_done, 1)

        def reciprocals(u, b):
            dve.wait_ge(s.exp_done, at(b, NU, u + 1))
            nc.vector.reciprocal(inv[:, u % PROBS, :], sums[:, u % PROBS, :]).then_inc(s.inv_done, 1)

        def step(b, attend, project, finish):
            p = nxt(b)
            if not attend:
                if project:
                    for t in range(TOK):
                        normalise(t, p)
                    for j in range(NP):
                        low(j, p)
                if finish:
                    for t in range(TOK):
                        add_out(t, prv(b))
                    for t in range(TOK):
                        take_stats(t, prv(b))
                return
            for t in range(SLOTS + 1):
                buf = b[1] % mask_bufs
                if t < NU:
                    dve.wait_ge(s.scores_done, at(b, NU, t + 1))
                    wait(dve, s.turned, at(b, NU, t + 1 - PROBS))
                    if t == 0:
                        dve.wait_ge(s.offset_in, 1 if mask_kind == "shared" else at(b, 1, 1))
                    if multiply:
                        nc.vector.tensor_tensor(prob[:, t % PROBS, :, :].rearrange("p t n -> p (t n)"), score_bank[t % 2][:, :],
                                                masks[:, buf, :, :].rearrange("p t n -> p (t n)"), ALU.mult).then_inc(s.masked, 1)
                if multiply and 1 <= t <= NU:
                    reciprocals(t - 1, b)
                if t < NU:
                    if multiply:
                        dve.wait_ge(s.masked, at(b, NU, t + 1))
                    dve.sem_inc(s.dve_passed, 1)
                    for h in range(TOK):
                        src = prob[:, t % PROBS, h, :] if multiply else score_bank[t % 2][:, h * TOKENS:(h + 1) * TOKENS]
                        ins = nc.vector.tensor_tensor_reduce(out=prob[:, t % PROBS, h, :], in0=src, in1=offset[:, buf, h, :],
                                                             scale=1.0, scalar=BIG, op0=ALU.add, op1=ALU.min,
                                                             accum_out=neg_max[:, t % PROBS, h:h + 1])
                    ins.then_inc(s.maxed, 1)
                if not multiply and 1 <= t <= NU:
                    reciprocals(t - 1, b)
                u = t - LAG
                if small and 0 <= u < NU and u % 2 == 1:
                    dve.wait_ge(s.turned, at(b, NU, u + 1))
                    if u % QUAD < 2:
                        wait(dve, s.pv_done, at(b, NQ, u // QUAD - 1))
                    nc.vector.tensor_copy(prob_t[:, u % (2 * QUAD), :, :].rearrange("p t n -> p (t n)"),
                                          pt_bank[1][:, :]).then_inc(s.pt_odd, 1)
                if project and t < TOK:
                    normalise(t, p)
                if finish and t in (2, 3):
                    add_out(t - 2, prv(b))
                if finish and t in (3, 4):
                    take_stats(t - 3, prv(b))
                if project:
                    for j in uses_at(t - 1):
                        low(j, p)
                q = (t - 8) // QUAD if t >= 8 and (t - 8) % QUAD == 0 else None
                if q is not None and q < NQ and (q + 1) % QPG == 0:
                    g = q // QPG
                    dve.wait_ge(s.ctx_high, at(b, GROUPS, g + 1))
                    nc.vector.tensor_tensor(ctx_lo[:, g, :], ctx_bank[g % 2][:, 0:TOKENS], ctx_hi[:, g, :].bitcast(F32),
                                            ALU.subtract).then_inc(s.ctx_split, 1)

        over_batches(dve, step)


def aggregate(nc, shared, eps):
    stats, moments, mean, rstd = (shared[n] for n in ("stats", "moments", "mean", "rstd"))
    done = shared["moments_done"]
    for i in range(TILES):
        nc.vector.bn_aggr(moments[:, i, :], stats[:, i, :]).then_inc(done, 1)
    shared["n_moments"] += TILES
    nc.vector.wait_ge(done, shared["n_moments"])
    nc.vector.tensor_copy(mean[:, :], moments[:, :, 0])
    return nc.vector.tensor_scalar(rstd[:, :], moments[:, :, 1], eps, None, ALU.add)


def mlp_stage(nc, ctx, shared, w1, b1, w2, b2, norm):
    x, mean, rstd, stats, ident, banks = (shared[n] for n in ("x", "mean", "rstd", "stats", "ident", "banks"))
    F = w1.shape[1]
    FT = F // P
    PAIRS = FT // 2
    HELD = 4

    def sb(n, shape, dt=F32):
        return ctx.enter_context(nc.sbuf_tensor(f"mlp_{n}", shape, dt))

    w1_hi, w1_lo = sb("w1_hi", [P, KT, F], F32R), sb("w1_lo", [P, KT, F], F32R)
    w2_hi, w2_lo = sb("w2_hi", [P, FT, D], F32R), sb("w2_lo", [P, FT, D], F32R)
    xn = sb("xn", [P, TOK, D])
    xt_hi, xt_lo = sb("xt_hi", [P, KT, TOKENS], F32R), sb("xt_lo", [P, KT, TOKENS], F32R)
    ring = sb("ring", [P, STAGED, 2 * TOKENS])
    lin, act_in = ring[:, 0:2, :], ring[:, 2:4, :]
    hid_hi, hid_lo = sb("hid_hi", [P, HELD, 2 * TOKENS], F32R), sb("hid_lo", [P, HELD, 2 * TOKENS], F32R)
    b1_col, b2_row = sb("b1_col", [P, FT]), sb("b2_row", [P, D])
    n_scale, n_bias = sb("n_scale", [P, D]), sb("n_bias", [P, D])
    hid_bank, out_bank, turn_bank = banks[0:4], [banks[4], banks[7]], banks[5:7]
    s = semaphores(nc, ctx, "mlp", """
        const_in w_high w_split stats_in std_in rstd_in normed scaled affine turned high_done turn_split
        hid_done lin_done poly_done inner_done tanh_done gelu_done hid_high hid_split part_done
        x_biased out_added stats_done""",
                   w_in=[ctx.enter_context(nc.semaphore(f"mlp_w_in{i}")) for i in range(STAGED)])
    chunks = (list(chunks_of(w1, w1_hi, w1_lo, D, 0)) + list(chunks_of(w2, w2_hi, w2_lo, F, 0, 0.5)))
    block = ctx.enter_context(nc.Block())

    def over(eng, step):
        step((0, -1), False, True)
        step((0, 0), True, True)
        with eng.Fori(0, BATCHES // 2 - 1) as r:
            step((r, 1), True, True)
            step((r, 2), True, True)
        step((BATCHES // 2 - 1, 1), True, False)

    @block.sync
    def _(sp):
        for dst, src in ((b1_col[:, :], b1.rearrange("(j p) -> p j", p=P)), (b2_row[:, :], row_of(b2, D)),
                         (n_scale[:, :], row_of(norm[0], D)), (n_bias[:, :], row_of(norm[1], D))):
            sp.dma_start(dst, src, allow_slow_non_contiguous=True).then_inc(s.const_in, 16)
        load_chunks(sp, chunks, ring, s)

    @block.gpsimd
    def _(pool):
        pool.wait_ge(s.const_in, 64)

        def step(b, work, prepare):
            p = nxt(b)
            if prepare:
                for t in range(TOK):
                    pool.wait_ge(s.normed, at(p, TOK, t + 1))
                    nc.gpsimd.tensor_tensor(xn[:, t, :], xn[:, t, :], n_scale[:, :], ALU.mult).then_inc(s.scaled, 1)
                for t in range(TOK):
                    pool.wait_ge(s.scaled, at(p, TOK, t + 1))
                    nc.gpsimd.tensor_tensor(xn[:, t, :], xn[:, t, :], n_bias[:, :], ALU.add).then_inc(s.affine, 1)
                for t in range(TOK):
                    n = at(p, TOK, t)
                    tile = x[:, n:n + 1, :] if isinstance(n, int) else x[:, bass.ds(n, 1), :]
                    nc.gpsimd.tensor_tensor(tile, tile, b2_row[:, :].rearrange("p (a d) -> p a d", a=1),
                                            ALU.add).then_inc(s.x_biased, 1)

        over(pool, step)

    @block.scalar
    def _(act):
        high_chunks(nc, act, chunks, ring, s)
        act.wait_ge(s.stats_in, 1)
        nc.scalar.activation(rstd[:, :], rstd[:, :], ACT.Sqrt).then_inc(s.std_in, 1)
        act.wait_ge(s.const_in, 64)

        def turn_high(i, p):
            act.wait_ge(s.turned, at(p, 2, i + 1))
            nc.scalar.activation(xt_hi[:, 2 * i:2 * i + 2, :].rearrange("p k t -> p (k t)"), turn_bank[i][:, :],
                                 ACT.Copy).then_inc(s.high_done, 1)

        def tanh(n, b):
            act.wait_ge(s.inner_done, at(b, PAIRS, n + 1))
            nc.scalar.activation(act_in[:, n % 2, :], act_in[:, n % 2, :], ACT.Tanh).then_inc(s.tanh_done, 1)

        def step(b, work, prepare):
            p = nxt(b)
            if work:
                for n in range(PAIRS + 1):
                    if n < PAIRS:
                        act.wait_ge(s.hid_done, at(b, PAIRS, n + 1))
                        wait(act, s.hid_split, at(b, PAIRS, n - 1))
                        bank = hid_bank[n % 4]
                        for m in range(2):
                            c = slice(m * TOKENS, (m + 1) * TOKENS)
                            bias = b1_col[:, 2 * n + m:2 * n + m + 1]
                            nc.scalar.activation(lin[:, n % 2, c], bank[:, c], ACT.Identity, bias=bias)
                            ins = nc.scalar.activation(act_in[:, n % 2, c], bank[:, c], ACT.Square, bias=bias)
                        ins.then_inc(s.lin_done, 1)
                    if n >= 1:
                        tanh(n - 1, b)
            if prepare:
                for i in range(2):
                    turn_high(i, p)

        over(act, step)

    @block.tensor
    def _(pe):
        pe.wait_ge(s.w_split, len(chunks))

        def hidden(n, b):
            wait(pe, s.lin_done, at(b, PAIRS, n - 3))
            if n == 0:
                pe.wait_ge(s.turn_split, at(b, 2, 2))
            for m in range(2):
                c = (2 * n + m) * P
                for k in range(KT):
                    ins = passes(nc, hid_bank[n % 4][:, m * TOKENS:(m + 1) * TOKENS],
                                 (w1_hi[:, k, c:c + P], w1_lo[:, k, c:c + P]), (xt_hi[:, k, :], xt_lo[:, k, :]),
                                 k == 0, k == KT - 1)
            ins.then_inc(s.hid_done, 1)

        def out_part(n, b):
            pe.wait_ge(s.hid_split, at(b, PAIRS, n + 1))
            if n == 0:
                wait(pe, s.out_added, at(b, TOK))
            for t in range(TOK):
                for m in range(2):
                    k = 2 * n + m
                    c = m * TOKENS + t * P
                    ins = passes(nc, out_bank[t][:, :], (hid_hi[:, n % HELD, c:c + P], hid_lo[:, n % HELD, c:c + P]),
                                 (w2_hi[:, k, :], w2_lo[:, k, :]), k == 0, k == FT - 1)
            ins.then_inc(s.part_done, 1)

        def turn(i, p):
            wait(pe, s.turn_split, at(p, 2, i - 1))
            if i == 0:
                pe.wait_ge(s.affine, at(p, TOK, TOK))
            for kk in range(2):
                for t in range(TOK):
                    c, k = kk * TOKENS + t * P, 2 * i + kk
                    ins = nc.tensor.transpose(turn_bank[i][:, c:c + P], xn[:, t, k * P:(k + 1) * P], ident[:, :])
            ins.then_inc(s.turned, 1)

        def step(b, work, prepare):
            p = nxt(b)
            if work:
                for n in range(PAIRS):
                    hidden(n, b)
                    if n >= 2:
                        out_part(n - 2, b)
            if prepare:
                for i in range(2):
                    turn(i, p)
            if work:
                for n in range(PAIRS - 2, PAIRS):
                    out_part(n, b)

        over(pe, step)

    @block.vector
    def _(dve):
        aggregate(nc, shared, 1e-5).then_inc(s.stats_in, 1)
        low_chunks(nc, dve, chunks, ring, s)
        dve.wait_ge(s.std_in, 1)
        nc.vector.reciprocal(rstd[:, :], rstd[:, :]).then_inc(s.rstd_in, 1)
        dve.wait_ge(s.rstd_in, 1)

        def polynomial(n, b):
            a = act_in[:, n % 2, :]
            dve.wait_ge(s.lin_done, at(b, PAIRS, n + 1))
            nc.vector.tensor_scalar(a, a, GELU_C * GELU_A, GELU_C, ALU.mult, ALU.add).then_inc(s.poly_done, 1)
            dve.wait_ge(s.poly_done, at(b, PAIRS, n + 1))
            nc.vector.tensor_tensor(a, a, lin[:, n % 2, :], ALU.mult).then_inc(s.inner_done, 1)

        def gelu(n, b):
            u = lin[:, n % 2, :]
            dve.wait_ge(s.tanh_done, at(b, PAIRS, n + 1))
            nc.vector.scalar_tensor_tensor(out=u, in0=act_in[:, n % 2, :], scalar=1.0, in1=u, op0=ALU.add,
                                           op1=ALU.mult).then_inc(s.gelu_done, 1)
            wait(dve, s.part_done, at(b, PAIRS, n + 1 - HELD))
            dve.wait_ge(s.gelu_done, at(b, PAIRS, n + 1))
            nc.vector.tensor_copy(hid_hi[:, n % HELD, :], u).then_inc(s.hid_high, 1)
            dve.wait_ge(s.hid_high, at(b, PAIRS, n + 1))
            nc.vector.tensor_tensor(hid_lo[:, n % HELD, :], u, hid_hi[:, n % HELD, :].bitcast(F32),
                                    ALU.subtract).then_inc(s.hid_split, 1)

        def tile_of(arr, n):
            return arr[:, n:n + 1] if isinstance(n, int) else arr[:, bass.ds(n, 1)]

        def normalise(t, p):
            wait(dve, s.turned, at(p, 2))
            n = at(p, TOK, t)
            src = x[:, n:n + 1, :] if isinstance(n, int) else x[:, bass.ds(n, 1), :]
            nc.vector.tensor_scalar(xn[:, t:t + 1, :], src, tile_of(mean, n), tile_of(rstd, n), ALU.subtract,
                                    ALU.mult).then_inc(s.normed, 1)

        def step(b, work, prepare):
            p = nxt(b)
            if prepare:
                for t in range(TOK):
                    normalise(t, p)
            if work:
                for n in range(PAIRS + 1):
                    if n < PAIRS:
                        polynomial(n, b)
                    if n >= 1:
                        gelu(n - 1, b)
            if prepare:
                for i in range(2):
                    dve.wait_ge(s.high_done, at(p, 2, i + 1))
                    nc.vector.tensor_tensor(xt_lo[:, 2 * i:2 * i + 2, :].rearrange("p k t -> p (k t)"), turn_bank[i][:, :],
                                            xt_hi[:, 2 * i:2 * i + 2, :].rearrange("p k t -> p (k t)").bitcast(F32),
                                            ALU.subtract).then_inc(s.turn_split, 1)
            if work:
                dve.wait_ge(s.part_done, at(b, PAIRS, PAIRS))
                dve.wait_ge(s.x_biased, at(b, TOK, TOK))
                for t in range(TOK):
                    n = at(b, TOK, t)
                    tile = x[:, n:n + 1, :] if isinstance(n, int) else x[:, bass.ds(n, 1), :]
                    nc.vector.tensor_tensor(tile, out_bank[t][:, :].rearrange("p (a d) -> p a d", a=1), tile,
                                            ALU.add).then_inc(s.out_added, 1)

        over(dve, step)


def last_norm(nc, ctx, shared, gamma, beta, out):
    x, mean, rstd = shared["x"], shared["mean"], shared["rstd"]
    scale = ctx.enter_context(nc.sbuf_tensor("last_scale", [P, D], F32))
    bias = ctx.enter_context(nc.sbuf_tensor("last_bias", [P, D], F32))
    s = semaphores(nc, ctx, "last", "const_in stats_in std_in rstd_in normed scaled shifted stored")
    block = ctx.enter_context(nc.Block())

    @block.sync
    def _(sp):
        sp.dma_start(scale[:, :], row_of(gamma, D)).then_inc(s.const_in, 16)
        sp.dma_start(bias[:, :], row_of(beta, D)).then_inc(s.const_in, 16)
        for i in range(TILES):
            b, t = divmod(i, TOK)
            sp.wait_ge(s.shifted, i + 1)
            sp.dma_start(out[b, t * P:(t + 1) * P, :], x[:, i, :]).then_inc(s.stored, 16)
        sp.wait_ge(s.stored, 16 * TILES)

    @block.scalar
    def _(act):
        act.wait_ge(s.stats_in, 1)
        nc.scalar.activation(rstd[:, :], rstd[:, :], ACT.Sqrt).then_inc(s.std_in, 1)

    @block.vector
    def _(dve):
        aggregate(nc, shared, 1e-6).then_inc(s.stats_in, 1)
        dve.wait_ge(s.std_in, 1)
        nc.vector.reciprocal(rstd[:, :], rstd[:, :]).then_inc(s.rstd_in, 1)
        dve.wait_ge(s.rstd_in, 1)
        dve.wait_ge(s.const_in, 32)
        for i in range(TILES + 1):
            if i < TILES:
                nc.vector.tensor_scalar(x[:, i, :], x[:, i, :], mean[:, i:i + 1], rstd[:, i:i + 1], ALU.subtract,
                                        ALU.mult).then_inc(s.normed, 1)
            if i >= 1:
                dve.wait_ge(s.normed, i)
                nc.vector.tensor_tensor(x[:, i - 1, :], x[:, i - 1, :], scale[:, :], ALU.mult).then_inc(s.scaled, 1)

    @block.gpsimd
    def _(pool):
        pool.wait_ge(s.const_in, 32)
        for i in range(TILES):
            pool.wait_ge(s.scaled, i + 1)
            nc.gpsimd.tensor_tensor(x[:, i, :], x[:, i, :], bias[:, :], ALU.add).then_inc(s.shifted, 1)


@contextmanager
def stage_of(nc):
    with ExitStack() as ctx:
        before = set(nc.free_semaphores)
        held = []
        with ExitStack() as inner:
            yield inner
            held = sorted(before - set(nc.free_semaphores))
        at_ = 0
        while at_ < len(held):
            end = at_
            while end + 1 < len(held) and held[end + 1] == held[end] + 1:
                end += 1
            nc.gpsimd.sem_clear(range(held[at_], held[end] + 1))
            at_ = end + 1
        nc.all_engine_barrier()


def build(nc, a, out):
    with ExitStack() as ctx:
        shared = {"x_dram": a["x"]}
        for n, shape in (("x", [P, TILES, D]), ("mean", [P, TILES]), ("rstd", [P, TILES]),
                         ("stats", [P, TILES, 6]), ("moments", [P, TILES, 2]), ("ident", [P, P])):
            shared[n] = ctx.enter_context(nc.sbuf_tensor(n, shape, F32))
        shared["banks"] = [ctx.enter_context(nc.psum_tensor(f"bank{i}", [P, 512], F32)) for i in range(8)]
        shared["ident_in"] = ctx.enter_context(nc.semaphore("ident_in"))
        shared["moments_done"] = ctx.enter_context(nc.semaphore("moments_done"))
        shared["n_moments"] = 0
        L0 = {k[len("L0_xattn_"):]: v for k, v in a.items() if k.startswith("L0_xattn_")}
        L1 = {k[len("L1_xattn_"):]: v for k, v in a.items() if k.startswith("L1_xattn_")}
        qkv, bqkv, kv, bkv = L0["w_qkv"], L0["b_qkv"], L0["w_kv"], L0["b_kv"]
        with stage_of(nc) as stage:
            attention_stage(nc, stage, "self", shared, out, q_src="x",
                            weights=(qkv[:, 0:D], qkv[:, D:2 * D], qkv[:, 2 * D:3 * D], L0["w_ao"]),
                            biases=(bqkv[0:D], bqkv[D:2 * D], bqkv[2 * D:3 * D], L0["b_ao"]),
                            norm=(L0["ln1_s"], L0["ln1_b"]), mask=a["mask_1x1xSxS2_fc1"], mask_kind="shared",
                            enc=None, heads=16, kv_heads=16, first_stage=True)
        with stage_of(nc) as stage:
            attention_stage(nc, stage, "cross", shared, out, q_src="x",
                            weights=(L0["w_q"], kv[:, 0:D], kv[:, D:2 * D], L0["w_co"]),
                            biases=(L0["b_q"], bkv[0:D], bkv[D:2 * D], L0["b_co"]),
                            norm=(L0["ln2_s"], L0["ln2_b"]), mask=a["mask_Bx1xSxS2_ff1"], mask_kind="batch",
                            enc=a["ctx_2048"], heads=16, kv_heads=16)
        with stage_of(nc) as stage:
            mlp_stage(nc, stage, shared, L0["w1"], L0["b1"], L0["w2"], L0["b2"], (L0["ln3_s"], L0["ln3_b"]))
        with stage_of(nc) as stage:
            attention_stage(nc, stage, "gqa", shared, out, q_src="x",
                            weights=(L1["Wq"], L1["Wk"], L1["Wv"], L1["Wo"]),
                            biases=(L1["bq"], L1["bk"], L1["bv"], L1["bo"]),
                            norm=None, mask=a["mask_Bx1xSxS2_ff0"], mask_kind="added",
                            enc=a["ctx_2048"], heads=32, kv_heads=8)
        with stage_of(nc) as stage:
            last_norm(nc, stage, shared, L1["gamma"], L1["beta"], out)


def kernel(**inputs):
    import numpy as _np
    import concourse.bacc as _bacc
    from concourse import mybir as _mybir
    from concourse.bass_utils import run_bass_kernel_spmd as _run

    nc = _bacc.Bacc("TRN2", target_bir_lowering=False, num_devices=1)
    arrays, args = {}, {}
    for name, value in inputs.items():
        a = _np.ascontiguousarray(value)
        arrays[f"in_{name}"] = a
        args[name] = nc.dram_tensor(f"in_{name}", a.shape, _mybir.dt.from_np(a.dtype), kind="ExternalInput").ap()
    out = nc.dram_tensor("out_rows", (BATCHES, TOKENS, D), F32, kind="ExternalOutput").ap()
    build(nc, args, out)
    r = _run(nc, [arrays], core_ids=[0])
    return r.results[0]["out_rows"]
```

```python
from collections import namedtuple
from contextlib import ExitStack, contextmanager

import concourse.bass as bass
import numpy as np
from concourse import mybir

F32 = mybir.dt.float32
F32R = mybir.dt.float32r
ALU = mybir.AluOpType
ACT = mybir.ActivationFunctionType

P = 128
BATCHES, TOKENS, D = 8, 256, 512
TOK = TOKENS // P
KT = D // P
TILES = BATCHES * TOK
GROUPS = D // P
QUAD = 4
ROWS = 32
STAGED = 4
BIG = 3.0e38
GELU_C, GELU_A = 0.7978845608028654, 0.044715


def at(batch, per, extra=0):
    r, k = batch
    return r * (2 * per) + (k * per + extra)


def wait(eng, sem, value):
    if not isinstance(value, int) or value > 0:
        eng.wait_ge(sem, value)


def passed(eng, sem, value, count):
    wait(eng, sem, value)
    if not isinstance(value, int):
        eng.sem_inc(count, 1)


def nxt(batch):
    return batch[0], batch[1] + 1


def prv(batch):
    return batch[0], batch[1] - 1


def over_batches(eng, step):
    step((0, -1), False, True, False)
    step((0, 0), True, True, False)
    with eng.Fori(0, (BATCHES - 2) // 2) as r:
        step((r, 1), True, True, True)
        step((r, 2), True, True, True)
    step((BATCHES // 2 - 1, 1), True, False, True)
    step((BATCHES // 2, 0), False, False, True)


def semaphores(nc, ctx, stage, names, **sets):
    sems = {name: ctx.enter_context(nc.semaphore(f"{stage}_{name}")) for name in names.split()}
    return namedtuple("Signals", [*sems, *sets])(**sems, **sets)


def passes(nc, out, stationary, moving, first, last):
    (sh, sl), (mh, ml) = stationary, moving
    nc.tensor.matmul(out, sh, mh, start=first, stop=False)
    nc.tensor.matmul(out, sh, ml, start=False, stop=False)
    return nc.tensor.matmul(out, sl, mh, start=False, stop=last)



def chunks_of(w, high, low, rows, at_col, scale=None):
    n = w.shape[1]
    for k in range(rows // P):
        for c in range(0, n, 512):
            m = min(512, n - c)
            yield (w[k * P:(k + 1) * P, c:c + m], high[:, k, at_col + c:at_col + c + m],
                   low[:, k, at_col + c:at_col + c + m], scale)


def load_chunks(sp, chunks, ring, s, start=0, end=None):
    for n, (src, _, _, _) in list(enumerate(chunks))[start:end]:
        wait(sp, s.w_split, n - STAGED + 1)
        sp.dma_start(ring[:, n % STAGED, 0:src.shape[1]], src).then_inc(s.w_in[n % STAGED], 16)


def landed(ring, n, shape):
    chunk = ring[:, n % STAGED, 0:int(np.prod(shape[1:]))]
    return chunk if len(shape) == 2 else chunk.rearrange("p (g c) -> p g c", g=shape[1])


def high_chunks(nc, act, chunks, ring, s, start=0, end=None):
    for n, (src, high, _, scale) in list(enumerate(chunks))[start:end]:
        act.wait_ge(s.w_in[n % STAGED], 16 * (n // STAGED + 1))
        nc.scalar.activation(high, landed(ring, n, high.shape), ACT.Copy,
                             scale=1.0 if scale is None else scale).then_inc(s.w_high, 1)


def low_chunks(nc, dve, chunks, ring, s, start=0, end=None):
    for n, (src, high, low, scale) in list(enumerate(chunks))[start:end]:
        dve.wait_ge(s.w_high, n + 1)
        nc.vector.scalar_tensor_tensor(out=low, in0=landed(ring, n, high.shape),
                                       scalar=1.0 if scale is None else scale, in1=high.bitcast(F32),
                                       op0=ALU.mult, op1=ALU.subtract).then_inc(s.w_split, 1)


def row_of(vector, n):
    return vector.rearrange("(a n) -> a n", a=1).broadcast_to([P, n])


def attention_stage(nc, ctx, name, shared, out, *, q_src, weights, biases, norm, mask, mask_kind,
                    enc, heads, kv_heads, first_stage=False):
    x, mean, rstd, stats, ident, banks = (shared[n] for n in ("x", "mean", "rstd", "stats", "ident", "banks"))
    HD = D // heads
    KVD = kv_heads * HD
    REP = heads // kv_heads
    K = 3 * ROWS
    NU = heads
    NQ = NU // QUAD
    EARLY_TILES = TOK * 2 if first_stage else TILES
    EARLY = 2
    PER_GROUP = P // HD
    CLASSES = P // ROWS
    HALF = NU // 2
    QPG = PER_GROUP // QUAD
    QS = -1.0 / float(np.sqrt(HD))
    multiply = mask_kind != "added"
    mask_bufs = 1 if mask_kind == "shared" else 2
    small = HD < 32
    LAG, PROBS = (4, 8) if small else (3, 4)
    MASK_SLOT = 7
    TAIL = LAG + 3

    def sb(n, shape, dt=F32):
        return ctx.enter_context(nc.sbuf_tensor(f"{name}_{n}", shape, dt))

    q_w, k_w, v_w, o_w = weights
    q_b, k_b, v_b, o_b = biases
    cols = {"q": 0, "k": D, "o": 2 * D, "v": 3 * D}
    NC = 3 * D + KVD
    w_hi, w_lo = sb("w_hi", [P, KT, NC], F32R), sb("w_lo", [P, KT, NC], F32R)
    xn = sb("xn", [P, TOK, D])
    xt_hi, xt_lo = sb("xt_hi", [P, KT, TOKENS], F32R), sb("xt_lo", [P, KT, TOKENS], F32R)
    part_slots = 4 if small else 2
    part_hi, part_lo = (sb(n, [P, part_slots, 2, TOKENS], F32R) for n in ("part_hi", "part_lo"))
    q_stack, k_stack = (sb(n, [K, D // ROWS, TOKENS], F32R) for n in ("q_stack", "k_stack"))
    value = sb("value", [P, 2, TOK, kv_heads, 3 * HD]) if small else sb("value", [P, 2, TOK, D])
    masks = sb("masks", [P, mask_bufs, TOK, TOKENS])
    offset = sb("offset", [P, mask_bufs, TOK, TOKENS]) if multiply else masks
    prob = sb("prob", [P, PROBS, TOK, TOKENS])
    ring = prob[:, :, :, :].rearrange("p s t n -> p s (t n)")
    neg_max, sums, inv = (sb(n, [P, PROBS, TOK]) for n in ("neg_max", "sums", "inv"))
    prob_t = sb("prob_t", [P, 2 * QUAD, TOK, TOKENS])
    ctx_hi, ctx_lo = sb("ctx_hi", [P, GROUPS, TOKENS], F32R), sb("ctx_lo", [P, GROUPS, TOKENS], F32R)
    q_bias, k_bias = sb("q_bias", [P, GROUPS]), sb("k_bias", [P, GROUPS])
    v_bias, o_bias = sb("v_bias", [P, KVD]), sb("o_bias", [P, D])
    if norm:
        n_scale, n_bias = sb("n_scale", [P, D]), sb("n_bias", [P, D])

    score_bank, pt_bank = banks[0:2], banks[2:4]
    ctx_bank, proj_bank = [banks[4], banks[7]], banks[5:7]

    def out_bank(t):
        return proj_bank[(out_at + t) % 2][:, :]


    w_in = [ctx.enter_context(nc.semaphore(f"{name}_w_in{i}")) for i in range(STAGED)]
    enc_loaded = [ctx.enter_context(nc.semaphore(f"{name}_enc_loaded{t}")) for t in range(TOK)]
    stacked = {}
    s = semaphores(nc, ctx, name, """
        const_in w_high w_split x_first x_in neg_bias value_zero stats_in std_in rstd_in
        x_stats normed scaled affine mask_loaded offset_in
        proj_done high_done proj_free scores_done masked k_bias_zero weight_zero maxed exp_done inv_done prob_done
        turned pt_even pt_odd pv_done ctx_high ctx_split out_done x_biased out_added stats_done
        sp_passed dve_passed""", w_in=w_in, enc_loaded=enc_loaded, stacked=stacked)

    if small:
        table = [("turn_x", 0, 3, 3, None), ("turn_x", 1, 4, 4, None), ("q", 0, 6, 7, 0), ("q", 1, 8, 9, 1),
                 ("turn_enc", 0, 10, 10, None), ("turn_enc", 1, 12, 12, None), ("k", 0, 17, 19, 2),
                 ("k", 1, 21, 23, 3), ("v", 0, 24, 25, None), ("v", 1, 26, 27, None)]
        out_slots, out_at, ctx_slots = (12, 13, 14, 15), 6, (17, 21, 29, 37)
    elif enc is not None:
        table = [("turn_x", 0, 3, 3, None), ("turn_x", 1, 4, 4, None), ("q", 0, 5, 6, 0), ("q", 1, 7, 8, 1),
                 ("turn_enc", 0, 9, 9, None), ("turn_enc", 1, 9, 9, None), ("k", 0, 10, 11, 0),
                 ("k", 1, 14, 15, 0), ("v", 0, 16, 17, None), ("v", 1, 17, 18, None)]
        out_slots, out_at, ctx_slots = (11, 12, 12, 13), 7, (14, 15, 17, 20)
    else:
        table = [("turn_x", 0, 3, 3, None), ("turn_x", 1, 4, 4, None), ("k", 0, 5, 6, 0), ("q", 0, 7, 8, 1),
                 ("k", 1, 12, 13, 0), ("q", 1, 14, 15, 1), ("v", 0, 16, 17, None), ("v", 1, 17, 18, None)]
        out_slots, out_at, ctx_slots = (9, 10, 11, 12), 4, (13, 14, 16, 20)
    uses = [u[:2] for u in table]
    halves = [u[2:4] for u in table]
    part_slot = {u[:2]: u[4] for u in table if u[4] is not None}
    NP = len(uses)
    left_at = [u[3] + (0 if "turn" in u[0] else 1) for u in table]
    assert all(a <= b for a, b in zip(left_at, left_at[1:])) and left_at[-1] <= left_at[0] + NU
    assert NP % 2 == 0
    index = {u: j for j, u in enumerate(uses)}
    highs = [u for u in uses if u[0] != "v"]
    NH = len(highs)
    parts = [u for u in uses if u[0] in "qk"]
    order = sorted(parts, key=lambda u: (u[1], index[u]))
    stacked.update({u: ctx.enter_context(nc.semaphore(f"{name}_stacked_{u[0]}{u[1]}")) for u in parts})
    N_DMA = 3 * CLASSES
    N_CONST = 7 if small else 6 if norm else 4

    def in_slot(t, slot, b, attend, finish):
        if slot == t and attend:
            return [b]
        if slot == t + NU and finish:
            return [prv(b)]
        return []

    def halves_at(t, b, project, attend):
        late = [(j, half, b) for j in range(NP) for half in range(2) if halves[j][half] == t + NU and attend]
        return late + [(j, half, nxt(b)) for j in range(NP) for half in range(2) if halves[j][half] == t and project]

    def evacuated_at(t, b, project, attend):
        late = [(j, b) for j in range(NP) if left_at[j] == t + NU and attend]
        return late + [(j, nxt(b)) for j in range(NP) if left_at[j] == t and project]

    def unit_at(t, lag, b, attend, finish):
        if t >= lag:
            return [(t - lag, b)] if attend else []
        return [(t - lag + NU, prv(b))] if finish else []

    def head_of(u):
        if not small:
            return u
        g, r = divmod(u, PER_GROUP)
        return g * PER_GROUP + 2 * (r % QUAD) + r // QUAD

    key_order = list(dict.fromkeys(u[0] for u in uses if u[0] in "qkv")) + ["o"]
    w_of = {"q": q_w, "k": k_w, "v": v_w, "o": o_w}
    chunks, chunk_end, chunk_start = [], {}, {}
    for key in key_order:
        chunk_start[key] = len(chunks)
        if small and key == "k":
            for k in range(KT):
                views = [part[:, k, D:2 * D].rearrange("p (g c) -> p g c", g=kv_heads) for part in (w_hi, w_lo)]
                for c in (0, 3 * HD):
                    chunks.append((k_w[k * P:(k + 1) * P, :], views[0][:, :, c:c + HD], views[1][:, :, c:c + HD], None))
        else:
            chunks += list(chunks_of(w_of[key], w_hi, w_lo, D, cols[key], QS if key == "q" else None))
        chunk_end[key] = len(chunks)
    split_before = {0: [key_order[0]]}
    for key, nxt_key in zip(key_order, key_order[1:]):
        split_before.setdefault(index[(key, 0)], []).append(nxt_key)

    def w_part(key, k, a, b):
        c = cols[key]
        return w_hi[:, k, c + a:c + b], w_lo[:, k, c + a:c + b]

    block = ctx.enter_context(nc.Block())

    @block.sync
    def _(sp):
        small_in = [(q_bias[:, :], q_b.rearrange("(j p) -> p j", p=P)),
                    (v_bias[:, :], row_of(v_b, KVD)), (o_bias[:, :], row_of(o_b, D))]
        if small:
            sp.wait_ge(s.k_bias_zero, 1)
            for half in range(2):
                for c in (0, 3 * HD):
                    small_in.append((k_bias[64 * half + c:64 * half + c + HD, :],
                                     k_b.rearrange("(j g d) -> g d j", g=2, d=HD)[half]))
        else:
            small_in.append((k_bias[:, :], k_b.rearrange("(j p) -> p j", p=P)))
        if norm:
            small_in += [(n_scale[:, :], row_of(norm[0], D)), (n_bias[:, :], row_of(norm[1], D))]

        def load_x(b):
            sp.dma_start(x[:, TOK * b:TOK * (b + 1), :], shared["x_dram"][b].rearrange("(t p) d -> p t d", p=P)
                         ).then_inc(s.x_first if b < EARLY else s.x_in, 16)

        if first_stage:
            for b in range(EARLY):
                load_x(b)
        load_chunks(sp, chunks, ring, s, 0, chunk_end[key_order[0]])
        for dst, src in small_in:
            sp.dma_start(dst, src, allow_slow_non_contiguous=True).then_inc(s.const_in, 16)

        def load_enc(b, t):
            rows = enc.rearrange("b (t p) d -> (b t) p d", p=P)
            n = at(b, TOK, t)
            src = rows[n] if isinstance(n, int) else rows[bass.ds(n, 1)].rearrange("a p d -> (a p) d")
            passed(sp, s.proj_done, at(b, NP, index[("turn_x", t)] + 1), s.sp_passed)
            sp.dma_start(xn[:, t, :], src).then_inc(s.enc_loaded[t], 16)

        def load_mask(b):
            n = at(b, 1)
            src = mask[0:1] if mask_kind == "shared" else mask[bass.ds(n, 1)] if not isinstance(n, int) else mask[n:n + 1]
            sp.dma_start(masks[:, b[1] % mask_bufs, :, :],
                         src.rearrange("a b (t p) n -> p (a b t) n", p=P)).then_inc(s.mask_loaded, 16)

        def stack(u, p):
            passed(sp, s.proj_free, at(p, NP, index[u] + 1), s.sp_passed)
            passed(sp, s.scores_done, at(prv(p), NU, (u[1] + 1) * HALF), s.sp_passed)
            stack_of = q_stack if u[0] == "q" else k_stack
            for r in range(CLASSES):
                for part in range(3):
                    low = part == (1 if u[0] == "q" else 2)
                    src = (part_lo if low else part_hi)[r * ROWS:(r + 1) * ROWS, part_slot[u], :, :]
                    g = 2 * CLASSES * u[1] + r
                    dst = stack_of[part * ROWS:(part + 1) * ROWS, g:g + CLASSES + 1:CLASSES, :]
                    sp.dma_start(dst.bitcast(F32), src.bitcast(F32)).then_inc(s.stacked[u], 16)

        def step(b, attend, project, finish):
            if not project:
                return
            p = nxt(b)
            if not attend:
                load_mask(p)
                load_chunks(sp, chunks, ring, s, chunk_end[key_order[0]], chunk_end[key_order[1]])
                if first_stage:
                    for n in range(EARLY, BATCHES):
                        load_x(n)
                if enc is not None:
                    for t in range(TOK):
                        load_enc(p, t)
                load_chunks(sp, chunks, ring, s, chunk_end[key_order[1]], chunk_end[key_order[2]])
                stack(order[0], p)
                load_chunks(sp, chunks, ring, s, chunk_end[key_order[2]], None)
                for u in order[1:]:
                    stack(u, p)
                return
            if mask_kind != "shared":
                passed(sp, s.maxed, at(b, NU, 0), s.sp_passed)
                load_mask(p)
            if enc is not None:
                for t in range(TOK):
                    load_enc(p, t)
            for u in order:
                stack(u, p)

        over_batches(sp, step)

    @block.gpsimd
    def _(pool):
        if first_stage:
            nc.gpsimd.memset(ident[:, :], 0.0).then_inc(shared["ident_in"], 1)
            pool.wait_ge(shared["ident_in"], 1)
            nc.gpsimd.affine_select(out=ident[:, :], in_=ident[:, :], compare_op=ALU.not_equal, fill=1.0,
                                    base=0, pattern=[[-1, P]], channel_multiplier=1).then_inc(shared["ident_in"], 1)
        if small:
            nc.gpsimd.memset(k_bias[:, :], 0.0).then_inc(s.k_bias_zero, 1)
            nc.gpsimd.memset(w_hi[:, :, D:2 * D].bitcast(F32), 0.0).then_inc(s.weight_zero, 1)
            nc.gpsimd.memset(w_lo[:, :, D:2 * D].bitcast(F32), 0.0).then_inc(s.weight_zero, 1)
            nc.gpsimd.memset(value[:, :, :, :, :], 0.0).then_inc(s.value_zero, 1)
        pool.wait_ge(s.const_in, 16 * N_CONST)
        nc.gpsimd.tensor_scalar(q_bias[:, :], q_bias[:, :], QS, None, ALU.mult).then_inc(s.neg_bias, 1)

        def affine(p, i):
            t = i // 2
            if i % 2 == 0:
                pool.wait_ge(s.normed, at(p, TOK, t + 1))
                nc.gpsimd.tensor_tensor(xn[:, t, :], xn[:, t, :], n_scale[:, :], ALU.mult).then_inc(s.scaled, 1)
            else:
                pool.wait_ge(s.scaled, at(p, TOK, t + 1))
                nc.gpsimd.tensor_tensor(xn[:, t, :], xn[:, t, :], n_bias[:, :], ALU.add).then_inc(s.affine, 1)

        def bias_x(b):
            wait(pool, s.normed, at(b, TOK, TOK))
            for t in range(TOK):
                tile = x[:, bass.ds(at(b, TOK, t), 1), :] if not isinstance(at(b, 1), int) else x[:, at(b, TOK, t):at(b, TOK, t) + 1, :]
                nc.gpsimd.tensor_tensor(tile, tile, o_bias[:, :].rearrange("p (a d) -> p a d", a=1),
                                        ALU.add).then_inc(s.x_biased, 1)

        def step(b, attend, project, finish):
            p = nxt(b)
            if not attend and project:
                if norm:
                    for i in range(2 * TOK):
                        affine(p, i)
            for t in range(NU if attend else 1):
                for u, ub in unit_at(t, 1, b, attend, finish):
                    pool.wait_ge(s.inv_done, at(ub, NU, u + 1))
                    pr = prob[:, u % PROBS, :, :]
                    nc.gpsimd.tensor_tensor(pr, pr, inv[:, u % PROBS, :].rearrange("p (t a) -> p t a", a=1)
                                            .broadcast_to([P, TOK, TOKENS]), ALU.mult).then_inc(s.prob_done, 1)
                if norm and attend and project and t < 2 * TOK:
                    affine(p, t)
                if t == 8:
                    bias_x(b)

        over_batches(pool, step)

    @block.scalar
    def _(act):
        def roots(start, end, n):
            act.wait_ge(s.stats_in, n)
            nc.scalar.activation(rstd[:, start:end], rstd[:, start:end], ACT.Sqrt).then_inc(s.std_in, 1)

        if small:
            act.wait_ge(s.weight_zero, 2)
        if norm:
            roots(0, EARLY_TILES, 1)

        def high(j, p):
            u = uses[j]
            bank = proj_bank[j % 2]
            act.wait_ge(s.proj_done, at(p, NP, j + 1))
            if u[0] in ("turn_x", "turn_enc"):
                nc.scalar.activation(xt_hi[:, :, u[1] * P:(u[1] + 1) * P], bank[:, :].rearrange("p (k t) -> p k t", k=KT),
                                     ACT.Copy).then_inc(s.high_done, 1)
                return
            slot = part_slot[u]
            same = [v for v in parts if part_slot[v] == slot]
            v = same[same.index(u) - 1]
            wait(act, s.stacked[v], at(p if index[v] < index[u] else prv(p), 16 * N_DMA, 16 * N_DMA))
            bias = q_bias if u[0] == "q" else k_bias
            if isinstance(p[0], int) and p == (0, 0):
                act.wait_ge(s.neg_bias, 1)
            for m in range(2):
                ins = nc.scalar.activation(part_hi[:, slot, m, :], bank[:, m * TOKENS:(m + 1) * TOKENS], ACT.Identity,
                                           bias=bias[:, 2 * u[1] + m:2 * u[1] + m + 1])
            ins.then_inc(s.high_done, 1)

        def evacuate(u, b):
            act.wait_ge(s.turned, at(b, NU, u + 1))
            if u % QUAD < 2:
                wait(act, s.pv_done, at(b, NQ, u // QUAD - 1))
            nc.scalar.activation(prob_t[:, u % (2 * QUAD), :, :].rearrange("p t n -> p (t n)"), pt_bank[u % 2][:, :],
                                 ACT.Copy).then_inc(s.pt_odd if u % 2 else s.pt_even, 1)

        def exponentials(u, b):
            act.wait_ge(s.maxed, at(b, NU, u + 1))
            for h in range(TOK):
                pr = prob[:, u % PROBS, h, :]
                ins = nc.scalar.activation(pr, pr, ACT.Exp, bias=neg_max[:, u % PROBS, h:h + 1], scale=-1.0,
                                           accum_out=sums[:, u % PROBS, h:h + 1])
            ins.then_inc(s.exp_done, 1)

        def context_high(g, b):
            act.wait_ge(s.pv_done, at(b, NQ, (g + 1) * QPG))
            wait(act, s.out_done, at(b, TOK))
            nc.scalar.activation(ctx_hi[:, g, :], ctx_bank[g % 2][:, 0:TOKENS], ACT.Copy).then_inc(s.ctx_high, 1)

        def step(b, attend, project, finish):
            if not attend and project:
                for j in range(NP):
                    for key in split_before.get(j, []):
                        high_chunks(nc, act, chunks, ring, s, chunk_start[key], chunk_end[key])
                    if uses[j] in highs and left_at[j] < NU:
                        high(j, nxt(b))
                return
            for t in range(NU if attend else TAIL):
                for u, ub in unit_at(t, LAG, b, attend, finish):
                    if not small or u % 2 == 0:
                        evacuate(u, ub)
                for j, p in evacuated_at(t, b, project, attend):
                    if uses[j] in highs:
                        high(j, p)
                for g in range(GROUPS):
                    for gb in in_slot(t, ctx_slots[g], b, attend, finish):
                        context_high(g, gb)
                if attend:
                    exponentials(t, b)
                if first_stage and attend and not finish and t == NU - 1:
                    roots(EARLY_TILES, TILES, 2)

        over_batches(act, step)

    @block.tensor
    def _(pe):
        if first_stage:
            pe.wait_ge(shared["ident_in"], 2)

        def project_use(j, half, p):
            u = uses[j]
            bank = proj_bank[j % 2]
            if half == 0:
                wait(pe, s.proj_free, at(p, NP, j - 1))
                if out_at <= j < out_at + TOK:
                    wait(pe, s.out_added, at(prv(prv(p)), TOK, j - out_at + 1))
            if u[0] in ("turn_x", "turn_enc"):
                if half == 1:
                    return
                t = u[1]
                if u[0] == "turn_x":
                    pe.wait_ge(s.affine if norm else s.normed, at(p, TOK, t + 1))
                    src = xn[:, t, :]
                else:
                    pe.wait_ge(s.enc_loaded[t], at(p, 16, 16))
                    src = xn[:, t, :]
                for k in range(KT):
                    ins = nc.tensor.transpose(bank[:, k * P:(k + 1) * P], src[:, k * P:(k + 1) * P], ident[:, :])
                ins.then_inc(s.proj_done, 1)
                return
            if half == 0:
                turned = index[("turn_enc" if enc is not None and u[0] in "kv" else "turn_x", 1)]
                pe.wait_ge(s.proj_free, at(p, NP, turned + 1))
                if isinstance(p[0], int) and p == (0, 0):
                    pe.wait_ge(s.w_split, chunk_end[u[0]])
            if u[0] == "v":
                for k in range(half * KT // 2, (half + 1) * KT // 2):
                    rows = xt_hi[:, k, u[1] * P:(u[1] + 1) * P], xt_lo[:, k, u[1] * P:(u[1] + 1) * P]
                    ins = passes(nc, bank[:, 0:KVD], rows, w_part("v", k, 0, KVD), k == 0, k == KT - 1)
            else:
                c = (2 * u[1] + half) * P
                for k in range(KT):
                    ins = passes(nc, bank[:, half * TOKENS:(half + 1) * TOKENS], w_part(u[0], k, c, c + P),
                                 (xt_hi[:, k, :], xt_lo[:, k, :]), k == 0, k == KT - 1)
            if half == 1:
                ins.then_inc(s.proj_done, 1)

        def scores(u, b):
            h = head_of(u)
            wait(pe, s.masked if multiply else s.maxed, at(b, NU, u - 1))
            if u % HALF == 0:
                for key in "qk":
                    pe.wait_ge(s.stacked[(key, u // HALF)], at(b, 16 * N_DMA, 16 * N_DMA))
            q_group = h * HD // ROWS
            k_group = h // REP * 2 + h % 2 if small else h
            for t in range(TOK):
                ins = nc.tensor.matmul(score_bank[u % 2][:, t * TOKENS:(t + 1) * TOKENS],
                                       q_stack[:, q_group, t * P:(t + 1) * P], k_stack[:, k_group, :],
                                       start=True, stop=True)
            ins.then_inc(s.scores_done, 1)

        def turn(u, b):
            pe.wait_ge(s.prob_done, at(b, NU, u + 1))
            wait(pe, s.pt_odd if u % 2 else s.pt_even, at(b, NU // 2, u // 2))
            for kt in range(TOK):
                for t in range(TOK):
                    c = kt * TOKENS + t * P
                    ins = nc.tensor.transpose(pt_bank[u % 2][:, c:c + P], prob[:, u % PROBS, t, kt * P:(kt + 1) * P], ident[:, :])
            ins.then_inc(s.turned, 1)

        def times_values(q, b):
            g = q // QPG
            pe.wait_ge(s.pt_even, at(b, NU // 2, 2 * (q + 1)))
            pe.wait_ge(s.pt_odd, at(b, NU // 2, 2 * (q + 1)))
            if q == 0:
                last_v = max(index[u] for u in uses if u[0] == "v")
                pe.wait_ge(s.proj_free, at(b, NP, last_v + 1))
            if q % QPG == 0:
                wait(pe, s.ctx_split, at(b, GROUPS, g - 1))
            first, last = q % QPG == 0, q % QPG == QPG - 1
            for kt in range(TOK):
                for i in range(QUAD):
                    u = q * QUAD + i
                    h = head_of(u)
                    if small:
                        c = HD * (1 - q % 2)
                        v = value[:, b[1] % 2, kt, h // REP, c:c + 2 * HD]
                    else:
                        v = value[:, b[1] % 2, kt, h * HD:(h + 1) * HD]
                    ins = nc.tensor.matmul(ctx_bank[g % 2][32 * i:32 * i + 32, 0:TOKENS], v, prob_t[:, u % (2 * QUAD), kt, :],
                                           start=first and kt == 0, stop=last and kt == TOK - 1)
            ins.then_inc(s.pv_done, 1)

        def project_out(t, half, b, p, projecting):
            if half == 0:
                if t == 0:
                    pe.wait_ge(s.ctx_split, at(b, GROUPS, GROUPS))
                    if not projecting:
                        pe.wait_ge(s.proj_free, NP * BATCHES)
                if projecting:
                    pe.wait_ge(s.proj_free, at(p, NP, out_at - 1 + t))
                else:
                    wait(pe, s.out_added, at(b, TOK, t + 1 - TOK))
            for k in range(half * KT // 2, (half + 1) * KT // 2):
                rows = ctx_hi[:, k, t * P:(t + 1) * P], ctx_lo[:, k, t * P:(t + 1) * P]
                ins = passes(nc, out_bank(t), rows, w_part("o", k, 0, D), k == 0, k == KT - 1)
            if half == 1:
                ins.then_inc(s.out_done, 1)

        def step(b, attend, project, finish):
            if not attend and project:
                for j in range(NP):
                    for half in range(2):
                        if halves[j][half] < NU:
                            project_use(j, half, nxt(b))
                pe.wait_ge(s.w_split, len(chunks))
                scores(0, nxt(b))
                return
            for t in range(NU if attend else TAIL):
                for u, ub in unit_at(t, LAG, b, attend, finish):
                    turn(u, ub)
                for q in range(NQ):
                    for qb in in_slot(t, LAG + QUAD * (q + 1), b, attend, finish):
                        times_values(q, qb)
                if attend and t + 1 < NU:
                    scores(t + 1, b)
                elif attend and project:
                    scores(0, nxt(b))
                for i, slot in enumerate(out_slots):
                    if slot == t and finish and attend:
                        project_out(i // 2, i % 2, prv(b), nxt(b), project)
                for j, half, p in halves_at(t, b, project, attend):
                    project_use(j, half, p)
            if not attend:
                for i in range(2 * TOK):
                    project_out(i // 2, i % 2, prv(b), None, False)

        over_batches(pe, step)

    @block.vector
    def _(dve):
        def first_stats(start, end):
            for i in range(start, end):
                nc.vector.bn_stats(stats[:, i, :], x[:, i, :]).then_inc(s.x_stats, 1)

        def inverse_roots(start, end, n):
            dve.wait_ge(s.std_in, n)
            nc.vector.reciprocal(rstd[:, start:end], rstd[:, start:end]).then_inc(s.rstd_in, 1)
            dve.wait_ge(s.rstd_in, n)

        if norm:
            if first_stage:
                dve.wait_ge(s.x_first, 16 * EARLY)
                first_stats(0, TOK * EARLY)
                dve.wait_ge(s.x_stats, TOK * EARLY)
            aggregate(nc, shared, 1e-5, 0, EARLY_TILES).then_inc(s.stats_in, 1)
            inverse_roots(0, EARLY_TILES, 1)
        if small:
            dve.wait_ge(s.value_zero, 1)

        def tile_of(arr, n):
            return arr[:, n:n + 1] if isinstance(n, int) else arr[:, bass.ds(n, 1)]

        def normalise(t, p):
            last = index[("turn_x" if enc is None else "turn_enc", 1)]
            wait(dve, s.proj_done, at(prv(p), NP, last + 1))
            n = at(p, TOK, t)
            src = x[:, n:n + 1, :] if isinstance(n, int) else x[:, bass.ds(n, 1), :]
            dst = xn[:, t:t + 1, :]
            if norm:
                ins = nc.vector.tensor_scalar(dst, src, tile_of(mean, n), tile_of(rstd, n), ALU.subtract, ALU.mult)
            else:
                ins = nc.vector.tensor_copy(dst, src)
            ins.then_inc(s.normed, 1)

        def offsets(p):
            buf = p[1] % mask_bufs
            dve.wait_ge(s.mask_loaded, at(p, 16, 16) if mask_kind != "shared" else 16)
            dve.sem_inc(s.dve_passed, 1)
            a, c = (1.0, -10000.0) if multiply else (0.0, -1.0)
            nc.vector.tensor_scalar(offset[:, buf, :, :], masks[:, buf, :, :], a, c, ALU.subtract,
                                    ALU.mult).then_inc(s.offset_in, 1)

        def low(j, p):
            u = uses[j]
            bank = proj_bank[j % 2]
            if u[0] == "v":
                dve.wait_ge(s.proj_done, at(p, NP, j + 1))
                if small:
                    ins = nc.vector.tensor_tensor(value[:, p[1] % 2, u[1], :, HD:2 * HD],
                                                  bank[:, 0:KVD].rearrange("p (h d) -> p h d", d=HD),
                                                  v_bias[:, :].rearrange("p (h d) -> p h d", d=HD), ALU.add)
                else:
                    ins = nc.vector.tensor_tensor(value[:, p[1] % 2, u[1], :], bank[:, :], v_bias[:, :], ALU.add)
                ins.then_inc(s.proj_free, 1)
                return
            dve.wait_ge(s.high_done, at(p, NH, highs.index(u) + 1))
            if u[0] in ("turn_x", "turn_enc"):
                c = slice(u[1] * P, (u[1] + 1) * P)
                nc.vector.tensor_tensor(xt_lo[:, :, c], bank[:, :].rearrange("p (k t) -> p k t", k=KT),
                                        xt_hi[:, :, c].bitcast(F32), ALU.subtract).then_inc(s.proj_free, 1)
                return
            slot = part_slot[u]
            bias = q_bias if u[0] == "q" else k_bias
            for m in range(2):
                ins = nc.vector.scalar_tensor_tensor(out=part_lo[:, slot, m, :], in0=bank[:, m * TOKENS:(m + 1) * TOKENS],
                                                     scalar=bias[:, 2 * u[1] + m:2 * u[1] + m + 1],
                                                     in1=part_hi[:, slot, m, :].bitcast(F32), op0=ALU.add, op1=ALU.subtract)
            ins.then_inc(s.proj_free, 1)

        def add_out(t, b):
            dve.wait_ge(s.out_done, at(b, TOK, t + 1))
            dve.wait_ge(s.x_biased, at(b, TOK, t + 1))
            n = at(b, TOK, t)
            tile = x[:, n:n + 1, :] if isinstance(n, int) else x[:, bass.ds(n, 1), :]
            nc.vector.tensor_tensor(tile, out_bank(t).rearrange("p (a d) -> p a d", a=1), tile,
                                    ALU.add).then_inc(s.out_added, 1)

        def take_stats(t, b):
            dve.wait_ge(s.out_added, at(b, TOK, t + 1))
            n = at(b, TOK, t)
            tile = x[:, n, :] if isinstance(n, int) else x[:, bass.ds(n, 1), :]
            st = stats[:, n, :] if isinstance(n, int) else stats[:, bass.ds(n, 1), :]
            nc.vector.bn_stats(st, tile).then_inc(s.stats_done, 1)

        def reciprocals(u, b):
            dve.wait_ge(s.exp_done, at(b, NU, u + 1))
            nc.vector.reciprocal(inv[:, u % PROBS, :], sums[:, u % PROBS, :]).then_inc(s.inv_done, 1)

        def mask_and_max(t, b):
            buf = b[1] % mask_bufs
            if multiply:
                dve.wait_ge(s.masked, at(b, NU, t + 1))
            dve.sem_inc(s.dve_passed, 1)
            for h in range(TOK):
                src = prob[:, t % PROBS, h, :] if multiply else score_bank[t % 2][:, h * TOKENS:(h + 1) * TOKENS]
                ins = nc.vector.tensor_tensor_reduce(out=prob[:, t % PROBS, h, :], in0=src, in1=offset[:, buf, h, :],
                                                     scale=1.0, scalar=BIG, op0=ALU.add, op1=ALU.min,
                                                     accum_out=neg_max[:, t % PROBS, h:h + 1])
            ins.then_inc(s.maxed, 1)

        def evacuate(u, b):
            dve.wait_ge(s.turned, at(b, NU, u + 1))
            if u % QUAD < 2:
                wait(dve, s.pv_done, at(b, NQ, u // QUAD - 1))
            nc.vector.tensor_copy(prob_t[:, u % (2 * QUAD), :, :].rearrange("p t n -> p (t n)"),
                                  pt_bank[1][:, :]).then_inc(s.pt_odd, 1)

        def context_low(g, b):
            dve.wait_ge(s.ctx_high, at(b, GROUPS, g + 1))
            nc.vector.tensor_tensor(ctx_lo[:, g, :], ctx_bank[g % 2][:, 0:TOKENS], ctx_hi[:, g, :].bitcast(F32),
                                    ALU.subtract).then_inc(s.ctx_split, 1)

        def step(b, attend, project, finish):
            if not attend and project:
                for t in range(TOK):
                    normalise(t, nxt(b))
                offsets(nxt(b))
                dve.wait_ge(s.const_in, 16 * N_CONST)
                dve.wait_ge(s.neg_bias, 1)
                for j in range(NP):
                    for key in split_before.get(j, []):
                        low_chunks(nc, dve, chunks, ring, s, chunk_start[key], chunk_end[key])
                    if left_at[j] < NU:
                        low(j, nxt(b))
                return
            for t in range(NU if attend else TAIL):
                if attend:
                    dve.wait_ge(s.scores_done, at(b, NU, t + 1))
                    wait(dve, s.turned, at(b, NU, t + 1 - PROBS))
                    if t == 0:
                        dve.wait_ge(s.offset_in, 1 if mask_kind == "shared" else at(b, 1, 1))
                    if multiply:
                        nc.vector.tensor_tensor(prob[:, t % PROBS, :, :].rearrange("p t n -> p (t n)"), score_bank[t % 2][:, :],
                                                masks[:, b[1] % mask_bufs, :, :].rearrange("p t n -> p (t n)"),
                                                ALU.mult).then_inc(s.masked, 1)
                if attend:
                    mask_and_max(t, b)
                for u, ub in unit_at(t, 1, b, attend, finish):
                    reciprocals(u, ub)
                for u, ub in unit_at(t, LAG, b, attend, finish):
                    if small and u % 2 == 1:
                        evacuate(u, ub)
                if project and attend and t < TOK:
                    normalise(t, nxt(b))
                if project and attend and t == MASK_SLOT and mask_kind != "shared":
                    offsets(nxt(b))
                if finish and attend:
                    for i in range(TOK):
                        if t == out_slots[2 * i + 1] + 1:
                            add_out(i, prv(b))
                        if t == out_slots[2 * i + 1] + 2:
                            take_stats(i, prv(b))
                for j, p in evacuated_at(t, b, project, attend):
                    low(j, p)
                for g in range(GROUPS):
                    for gb in in_slot(t, ctx_slots[g], b, attend, finish):
                        context_low(g, gb)
                if first_stage and attend and not finish:
                    i = TOK * EARLY + 2 * (t - 8)
                    if 8 <= t and i < TILES:
                        dve.wait_ge(s.x_in, 16 * (BATCHES - EARLY))
                        first_stats(i, i + 2)
                    if t == NU - 2:
                        dve.wait_ge(s.x_stats, TILES)
                        aggregate(nc, shared, 1e-5, EARLY_TILES, TILES).then_inc(s.stats_in, 1)
                    if t == NU - 1:
                        inverse_roots(EARLY_TILES, TILES, 2)
            if not attend:
                for t in range(TOK):
                    add_out(t, prv(b))
                for t in range(TOK):
                    take_stats(t, prv(b))

        over_batches(dve, step)


def aggregate(nc, shared, eps, start=0, end=TILES):
    stats, moments, mean, rstd = (shared[n] for n in ("stats", "moments", "mean", "rstd"))
    done = shared["moments_done"]
    for i in range(start, end):
        nc.vector.bn_aggr(moments[:, i, :], stats[:, i, :]).then_inc(done, 1)
    shared["n_moments"] += end - start
    nc.vector.wait_ge(done, shared["n_moments"])
    nc.vector.tensor_copy(mean[:, start:end], moments[:, start:end, 0])
    return nc.vector.tensor_scalar(rstd[:, start:end], moments[:, start:end, 1], eps, None, ALU.add)


def mlp_stage(nc, ctx, shared, w1, b1, w2, b2, norm):
    x, mean, rstd, stats, ident, banks = (shared[n] for n in ("x", "mean", "rstd", "stats", "ident", "banks"))
    F = w1.shape[1]
    FT = F // P
    PAIRS = FT // 2
    HELD = 4

    def sb(n, shape, dt=F32):
        return ctx.enter_context(nc.sbuf_tensor(f"mlp_{n}", shape, dt))

    w1_hi, w1_lo = sb("w1_hi", [P, KT, F], F32R), sb("w1_lo", [P, KT, F], F32R)
    w2_hi, w2_lo = sb("w2_hi", [P, FT, D], F32R), sb("w2_lo", [P, FT, D], F32R)
    xn = sb("xn", [P, TOK, D])
    xt_hi, xt_lo = sb("xt_hi", [P, KT, TOKENS], F32R), sb("xt_lo", [P, KT, TOKENS], F32R)
    ring = sb("ring", [P, STAGED, 2 * TOKENS])
    lin, act_in = ring[:, 0:2, :], ring[:, 2:4, :]
    hid_hi, hid_lo = sb("hid_hi", [P, HELD, 2 * TOKENS], F32R), sb("hid_lo", [P, HELD, 2 * TOKENS], F32R)
    b1_col, b2_row = sb("b1_col", [P, FT]), sb("b2_row", [P, D])
    n_scale, n_bias = sb("n_scale", [P, D]), sb("n_bias", [P, D])
    hid_bank, out_bank, turn_bank = banks[0:4], [banks[4], banks[7]], banks[5:7]
    s = semaphores(nc, ctx, "mlp", """
        const_in w_high w_split stats_in std_in rstd_in normed scaled affine turned high_done turn_split
        hid_done lin_done poly_done inner_done tanh_done gelu_done hid_high hid_split part_done
        x_biased out_added stats_done""",
                   w_in=[ctx.enter_context(nc.semaphore(f"mlp_w_in{i}")) for i in range(STAGED)])
    chunks = (list(chunks_of(w1, w1_hi, w1_lo, D, 0)) + list(chunks_of(w2, w2_hi, w2_lo, F, 0, 0.5)))
    block = ctx.enter_context(nc.Block())

    def over(eng, step):
        step((0, -1), False, True)
        step((0, 0), True, True)
        with eng.Fori(0, BATCHES // 2 - 1) as r:
            step((r, 1), True, True)
            step((r, 2), True, True)
        step((BATCHES // 2 - 1, 1), True, False)

    @block.sync
    def _(sp):
        for dst, src in ((b1_col[:, :], b1.rearrange("(j p) -> p j", p=P)), (b2_row[:, :], row_of(b2, D)),
                         (n_scale[:, :], row_of(norm[0], D)), (n_bias[:, :], row_of(norm[1], D))):
            sp.dma_start(dst, src, allow_slow_non_contiguous=True).then_inc(s.const_in, 16)
        load_chunks(sp, chunks, ring, s)

    @block.gpsimd
    def _(pool):
        pool.wait_ge(s.const_in, 64)

        def step(b, work, prepare):
            p = nxt(b)
            if prepare:
                for t in range(TOK):
                    pool.wait_ge(s.normed, at(p, TOK, t + 1))
                    nc.gpsimd.tensor_tensor(xn[:, t, :], xn[:, t, :], n_scale[:, :], ALU.mult).then_inc(s.scaled, 1)
                for t in range(TOK):
                    pool.wait_ge(s.scaled, at(p, TOK, t + 1))
                    nc.gpsimd.tensor_tensor(xn[:, t, :], xn[:, t, :], n_bias[:, :], ALU.add).then_inc(s.affine, 1)
                for t in range(TOK):
                    n = at(p, TOK, t)
                    tile = x[:, n:n + 1, :] if isinstance(n, int) else x[:, bass.ds(n, 1), :]
                    nc.gpsimd.tensor_tensor(tile, tile, b2_row[:, :].rearrange("p (a d) -> p a d", a=1),
                                            ALU.add).then_inc(s.x_biased, 1)

        over(pool, step)

    @block.scalar
    def _(act):
        high_chunks(nc, act, chunks, ring, s)
        act.wait_ge(s.stats_in, 1)
        nc.scalar.activation(rstd[:, :], rstd[:, :], ACT.Sqrt).then_inc(s.std_in, 1)
        act.wait_ge(s.const_in, 64)

        def turn_high(i, p):
            act.wait_ge(s.turned, at(p, 2, i + 1))
            nc.scalar.activation(xt_hi[:, 2 * i:2 * i + 2, :].rearrange("p k t -> p (k t)"), turn_bank[i][:, :],
                                 ACT.Copy).then_inc(s.high_done, 1)

        def tanh(n, b):
            act.wait_ge(s.inner_done, at(b, PAIRS, n + 1))
            nc.scalar.activation(act_in[:, n % 2, :], act_in[:, n % 2, :], ACT.Tanh).then_inc(s.tanh_done, 1)

        def step(b, work, prepare):
            p = nxt(b)
            if work:
                for n in range(PAIRS + 1):
                    if n < PAIRS:
                        act.wait_ge(s.hid_done, at(b, PAIRS, n + 1))
                        wait(act, s.hid_split, at(b, PAIRS, n - 1))
                        bank = hid_bank[n % 4]
                        for m in range(2):
                            c = slice(m * TOKENS, (m + 1) * TOKENS)
                            bias = b1_col[:, 2 * n + m:2 * n + m + 1]
                            nc.scalar.activation(lin[:, n % 2, c], bank[:, c], ACT.Identity, bias=bias)
                            ins = nc.scalar.activation(act_in[:, n % 2, c], bank[:, c], ACT.Square, bias=bias)
                        ins.then_inc(s.lin_done, 1)
                    if n >= 1:
                        tanh(n - 1, b)
            if prepare:
                for i in range(2):
                    turn_high(i, p)

        over(act, step)

    @block.tensor
    def _(pe):
        pe.wait_ge(s.w_split, len(chunks))

        def hidden(n, b):
            wait(pe, s.lin_done, at(b, PAIRS, n - 3))
            if n == 0:
                pe.wait_ge(s.turn_split, at(b, 2, 2))
            for m in range(2):
                c = (2 * n + m) * P
                for k in range(KT):
                    ins = passes(nc, hid_bank[n % 4][:, m * TOKENS:(m + 1) * TOKENS],
                                 (w1_hi[:, k, c:c + P], w1_lo[:, k, c:c + P]), (xt_hi[:, k, :], xt_lo[:, k, :]),
                                 k == 0, k == KT - 1)
            ins.then_inc(s.hid_done, 1)

        def out_part(n, b):
            pe.wait_ge(s.hid_split, at(b, PAIRS, n + 1))
            if n == 0:
                wait(pe, s.out_added, at(b, TOK))
            for t in range(TOK):
                for m in range(2):
                    k = 2 * n + m
                    c = m * TOKENS + t * P
                    ins = passes(nc, out_bank[t][:, :], (hid_hi[:, n % HELD, c:c + P], hid_lo[:, n % HELD, c:c + P]),
                                 (w2_hi[:, k, :], w2_lo[:, k, :]), k == 0, k == FT - 1)
            ins.then_inc(s.part_done, 1)

        def turn(i, p):
            wait(pe, s.turn_split, at(p, 2, i - 1))
            if i == 0:
                pe.wait_ge(s.affine, at(p, TOK, TOK))
            for kk in range(2):
                for t in range(TOK):
                    c, k = kk * TOKENS + t * P, 2 * i + kk
                    ins = nc.tensor.transpose(turn_bank[i][:, c:c + P], xn[:, t, k * P:(k + 1) * P], ident[:, :])
            ins.then_inc(s.turned, 1)

        def step(b, work, prepare):
            p = nxt(b)
            if work:
                for n in range(PAIRS):
                    hidden(n, b)
                    if n >= 2:
                        out_part(n - 2, b)
            if prepare:
                for i in range(2):
                    turn(i, p)
            if work:
                for n in range(PAIRS - 2, PAIRS):
                    out_part(n, b)

        over(pe, step)

    @block.vector
    def _(dve):
        aggregate(nc, shared, 1e-5).then_inc(s.stats_in, 1)
        low_chunks(nc, dve, chunks, ring, s)
        dve.wait_ge(s.std_in, 1)
        nc.vector.reciprocal(rstd[:, :], rstd[:, :]).then_inc(s.rstd_in, 1)
        dve.wait_ge(s.rstd_in, 1)

        def polynomial(n, b):
            a = act_in[:, n % 2, :]
            dve.wait_ge(s.lin_done, at(b, PAIRS, n + 1))
            nc.vector.tensor_scalar(a, a, GELU_C * GELU_A, GELU_C, ALU.mult, ALU.add).then_inc(s.poly_done, 1)
            dve.wait_ge(s.poly_done, at(b, PAIRS, n + 1))
            nc.vector.tensor_tensor(a, a, lin[:, n % 2, :], ALU.mult).then_inc(s.inner_done, 1)

        def gelu(n, b):
            u = lin[:, n % 2, :]
            dve.wait_ge(s.tanh_done, at(b, PAIRS, n + 1))
            nc.vector.scalar_tensor_tensor(out=u, in0=act_in[:, n % 2, :], scalar=1.0, in1=u, op0=ALU.add,
                                           op1=ALU.mult).then_inc(s.gelu_done, 1)
            wait(dve, s.part_done, at(b, PAIRS, n + 1 - HELD))
            dve.wait_ge(s.gelu_done, at(b, PAIRS, n + 1))
            nc.vector.tensor_copy(hid_hi[:, n % HELD, :], u).then_inc(s.hid_high, 1)
            dve.wait_ge(s.hid_high, at(b, PAIRS, n + 1))
            nc.vector.tensor_tensor(hid_lo[:, n % HELD, :], u, hid_hi[:, n % HELD, :].bitcast(F32),
                                    ALU.subtract).then_inc(s.hid_split, 1)

        def tile_of(arr, n):
            return arr[:, n:n + 1] if isinstance(n, int) else arr[:, bass.ds(n, 1)]

        def normalise(t, p):
            wait(dve, s.turned, at(p, 2))
            n = at(p, TOK, t)
            src = x[:, n:n + 1, :] if isinstance(n, int) else x[:, bass.ds(n, 1), :]
            nc.vector.tensor_scalar(xn[:, t:t + 1, :], src, tile_of(mean, n), tile_of(rstd, n), ALU.subtract,
                                    ALU.mult).then_inc(s.normed, 1)

        def step(b, work, prepare):
            p = nxt(b)
            if prepare:
                for t in range(TOK):
                    normalise(t, p)
            if work:
                for n in range(PAIRS + 1):
                    if n < PAIRS:
                        polynomial(n, b)
                    if n >= 1:
                        gelu(n - 1, b)
            if prepare:
                for i in range(2):
                    dve.wait_ge(s.high_done, at(p, 2, i + 1))
                    nc.vector.tensor_tensor(xt_lo[:, 2 * i:2 * i + 2, :].rearrange("p k t -> p (k t)"), turn_bank[i][:, :],
                                            xt_hi[:, 2 * i:2 * i + 2, :].rearrange("p k t -> p (k t)").bitcast(F32),
                                            ALU.subtract).then_inc(s.turn_split, 1)
            if work:
                dve.wait_ge(s.part_done, at(b, PAIRS, PAIRS))
                dve.wait_ge(s.x_biased, at(b, TOK, TOK))
                for t in range(TOK):
                    n = at(b, TOK, t)
                    tile = x[:, n:n + 1, :] if isinstance(n, int) else x[:, bass.ds(n, 1), :]
                    nc.vector.tensor_tensor(tile, out_bank[t][:, :].rearrange("p (a d) -> p a d", a=1), tile,
                                            ALU.add).then_inc(s.out_added, 1)

        over(dve, step)


def last_norm(nc, ctx, shared, gamma, beta, out):
    x, mean, rstd = shared["x"], shared["mean"], shared["rstd"]
    scale = ctx.enter_context(nc.sbuf_tensor("last_scale", [P, D], F32))
    bias = ctx.enter_context(nc.sbuf_tensor("last_bias", [P, D], F32))
    s = semaphores(nc, ctx, "last", "const_in stats_in std_in rstd_in normed scaled shifted stored")
    block = ctx.enter_context(nc.Block())

    @block.sync
    def _(sp):
        sp.dma_start(scale[:, :], row_of(gamma, D)).then_inc(s.const_in, 16)
        sp.dma_start(bias[:, :], row_of(beta, D)).then_inc(s.const_in, 16)
        for i in range(TILES):
            b, t = divmod(i, TOK)
            sp.wait_ge(s.shifted, i + 1)
            sp.dma_start(out[b, t * P:(t + 1) * P, :], x[:, i, :]).then_inc(s.stored, 16)
        sp.wait_ge(s.stored, 16 * TILES)

    @block.scalar
    def _(act):
        act.wait_ge(s.stats_in, 1)
        nc.scalar.activation(rstd[:, :], rstd[:, :], ACT.Sqrt).then_inc(s.std_in, 1)

    @block.vector
    def _(dve):
        aggregate(nc, shared, 1e-6).then_inc(s.stats_in, 1)
        dve.wait_ge(s.std_in, 1)
        nc.vector.reciprocal(rstd[:, :], rstd[:, :]).then_inc(s.rstd_in, 1)
        dve.wait_ge(s.rstd_in, 1)
        dve.wait_ge(s.const_in, 32)
        for i in range(TILES + 1):
            if i < TILES:
                nc.vector.tensor_scalar(x[:, i, :], x[:, i, :], mean[:, i:i + 1], rstd[:, i:i + 1], ALU.subtract,
                                        ALU.mult).then_inc(s.normed, 1)
            if i >= 1:
                dve.wait_ge(s.normed, i)
                nc.vector.tensor_tensor(x[:, i - 1, :], x[:, i - 1, :], scale[:, :], ALU.mult).then_inc(s.scaled, 1)

    @block.gpsimd
    def _(pool):
        pool.wait_ge(s.const_in, 32)
        for i in range(TILES):
            pool.wait_ge(s.scaled, i + 1)
            nc.gpsimd.tensor_tensor(x[:, i, :], x[:, i, :], bias[:, :], ALU.add).then_inc(s.shifted, 1)


@contextmanager
def stage_of(nc):
    with ExitStack() as ctx:
        before = set(nc.free_semaphores)
        held = []
        with ExitStack() as inner:
            yield inner
            held = sorted(before - set(nc.free_semaphores))
        at_ = 0
        while at_ < len(held):
            end = at_
            while end + 1 < len(held) and held[end + 1] == held[end] + 1:
                end += 1
            nc.gpsimd.sem_clear(range(held[at_], held[end] + 1))
            at_ = end + 1
        nc.all_engine_barrier()


def build(nc, a, out):
    with ExitStack() as ctx:
        shared = {"x_dram": a["x"]}
        for n, shape in (("x", [P, TILES, D]), ("mean", [P, TILES]), ("rstd", [P, TILES]),
                         ("stats", [P, TILES, 6]), ("moments", [P, TILES, 2]), ("ident", [P, P])):
            shared[n] = ctx.enter_context(nc.sbuf_tensor(n, shape, F32))
        shared["banks"] = [ctx.enter_context(nc.psum_tensor(f"bank{i}", [P, 512], F32)) for i in range(8)]
        shared["ident_in"] = ctx.enter_context(nc.semaphore("ident_in"))
        shared["moments_done"] = ctx.enter_context(nc.semaphore("moments_done"))
        shared["n_moments"] = 0
        L0 = {k[len("L0_xattn_"):]: v for k, v in a.items() if k.startswith("L0_xattn_")}
        L1 = {k[len("L1_xattn_"):]: v for k, v in a.items() if k.startswith("L1_xattn_")}
        qkv, bqkv, kv, bkv = L0["w_qkv"], L0["b_qkv"], L0["w_kv"], L0["b_kv"]
        with stage_of(nc) as stage:
            attention_stage(nc, stage, "self", shared, out, q_src="x",
                            weights=(qkv[:, 0:D], qkv[:, D:2 * D], qkv[:, 2 * D:3 * D], L0["w_ao"]),
                            biases=(bqkv[0:D], bqkv[D:2 * D], bqkv[2 * D:3 * D], L0["b_ao"]),
                            norm=(L0["ln1_s"], L0["ln1_b"]), mask=a["mask_1x1xSxS2_fc1"], mask_kind="shared",
                            enc=None, heads=16, kv_heads=16, first_stage=True)
        with stage_of(nc) as stage:
            attention_stage(nc, stage, "cross", shared, out, q_src="x",
                            weights=(L0["w_q"], kv[:, 0:D], kv[:, D:2 * D], L0["w_co"]),
                            biases=(L0["b_q"], bkv[0:D], bkv[D:2 * D], L0["b_co"]),
                            norm=(L0["ln2_s"], L0["ln2_b"]), mask=a["mask_Bx1xSxS2_ff1"], mask_kind="batch",
                            enc=a["ctx_2048"], heads=16, kv_heads=16)
        with stage_of(nc) as stage:
            mlp_stage(nc, stage, shared, L0["w1"], L0["b1"], L0["w2"], L0["b2"], (L0["ln3_s"], L0["ln3_b"]))
        with stage_of(nc) as stage:
            attention_stage(nc, stage, "gqa", shared, out, q_src="x",
                            weights=(L1["Wq"], L1["Wk"], L1["Wv"], L1["Wo"]),
                            biases=(L1["bq"], L1["bk"], L1["bv"], L1["bo"]),
                            norm=None, mask=a["mask_Bx1xSxS2_ff0"], mask_kind="added",
                            enc=a["ctx_2048"], heads=32, kv_heads=8)
        with stage_of(nc) as stage:
            last_norm(nc, stage, shared, L1["gamma"], L1["beta"], out)


def kernel(**inputs):
    import numpy as _np
    import concourse.bacc as _bacc
    from concourse import mybir as _mybir
    from concourse.bass_utils import run_bass_kernel_spmd as _run

    nc = _bacc.Bacc("TRN2", target_bir_lowering=False, num_devices=1)
    arrays, args = {}, {}
    for name, value in inputs.items():
        a = _np.ascontiguousarray(value)
        arrays[f"in_{name}"] = a
        args[name] = nc.dram_tensor(f"in_{name}", a.shape, _mybir.dt.from_np(a.dtype), kind="ExternalInput").ap()
    out = nc.dram_tensor("out_rows", (BATCHES, TOKENS, D), F32, kind="ExternalOutput").ap()
    build(nc, args, out)
    r = _run(nc, [arrays], core_ids=[0])
    return r.results[0]["out_rows"]
```

```python
from collections import namedtuple
from contextlib import ExitStack, contextmanager

import concourse.bass as bass
import numpy as np
from concourse import mybir

F32 = mybir.dt.float32
F32R = mybir.dt.float32r
ALU = mybir.AluOpType
ACT = mybir.ActivationFunctionType

P = 128
BATCHES, TOKENS, D = 8, 256, 512
TOK = TOKENS // P
KT = D // P
TILES = BATCHES * TOK
GROUPS = D // P
QUAD = 4
ROWS = 32
STAGED, MLP_STAGED = 8, 6
BIG = 3.0e38
GELU_C, GELU_A = 0.7978845608028654, 0.044715


def at(batch, per, extra=0):
    r, k = batch
    return r * (2 * per) + (k * per + extra)


def wait(eng, sem, value):
    if not isinstance(value, int) or value > 0:
        eng.wait_ge(sem, value)


def passed(eng, sem, value, count):
    wait(eng, sem, value)
    if not isinstance(value, int):
        eng.sem_inc(count, 1)


def nxt(batch):
    return batch[0], batch[1] + 1


def prv(batch):
    return batch[0], batch[1] - 1


def over_batches(eng, step):
    step((0, -1), False, True, False)
    step((0, 0), True, True, False)
    with eng.Fori(0, (BATCHES - 2) // 2) as r:
        step((r, 1), True, True, True)
        step((r, 2), True, True, True)
    step((BATCHES // 2 - 1, 1), True, False, True)
    step((BATCHES // 2, 0), False, False, True)


def semaphores(nc, ctx, stage, names, **sets):
    sems = {name: ctx.enter_context(nc.semaphore(f"{stage}_{name}")) for name in names.split()}
    return namedtuple("Signals", [*sems, *sets])(**sems, **sets)


def passes(nc, out, stationary, moving, first, last):
    (sh, sl), (mh, ml) = stationary, moving
    nc.tensor.matmul(out, sh, mh, start=first, stop=False)
    nc.tensor.matmul(out, sh, ml, start=False, stop=False)
    return nc.tensor.matmul(out, sl, mh, start=False, stop=last)



def chunks_of(w, high, low, rows, at_col, scale=None):
    n = w.shape[1]
    for k in range(rows // P):
        for c in range(0, n, 512):
            m = min(512, n - c)
            yield (w[k * P:(k + 1) * P, c:c + m], high[:, k, at_col + c:at_col + c + m],
                   low[:, k, at_col + c:at_col + c + m], scale)


def load_chunks(sp, chunks, ring, s, start=0, end=None):
    for n, (src, _, _, _) in list(enumerate(chunks))[start:end]:
        wait(sp, s.w_split, n - len(s.w_in) + 1)
        sp.dma_start(ring[:, n % len(s.w_in), 0:src.shape[1]], src).then_inc(s.w_in[n % len(s.w_in)], 16)


def landed(ring, n, shape, s):
    chunk = ring[:, n % len(s.w_in), 0:int(np.prod(shape[1:]))]
    return chunk if len(shape) == 2 else chunk.rearrange("p (g c) -> p g c", g=shape[1])


def high_chunks(nc, act, chunks, ring, s, start=0, end=None):
    for n, (src, high, _, scale) in list(enumerate(chunks))[start:end]:
        act.wait_ge(s.w_in[n % len(s.w_in)], 16 * (n // len(s.w_in) + 1))
        nc.scalar.activation(high, landed(ring, n, high.shape, s), ACT.Copy,
                             scale=1.0 if scale is None else scale).then_inc(s.w_high, 1)


def low_chunks(nc, dve, chunks, ring, s, start=0, end=None):
    for n, (src, high, low, scale) in list(enumerate(chunks))[start:end]:
        dve.wait_ge(s.w_high, n + 1)
        nc.vector.scalar_tensor_tensor(out=low, in0=landed(ring, n, high.shape, s),
                                       scalar=1.0 if scale is None else scale, in1=high.bitcast(F32),
                                       op0=ALU.mult, op1=ALU.subtract).then_inc(s.w_split, 1)


def row_of(vector, n):
    return vector.rearrange("(a n) -> a n", a=1).broadcast_to([P, n])


def attention_stage(nc, ctx, name, shared, out, *, q_src, weights, biases, norm, mask, mask_kind,
                    enc, heads, kv_heads, first_stage=False):
    x, mean, rstd, stats, ident, banks = (shared[n] for n in ("x", "mean", "rstd", "stats", "ident", "banks"))
    HD = D // heads
    KVD = kv_heads * HD
    REP = heads // kv_heads
    K = 3 * ROWS
    NU = heads
    NQ = NU // QUAD
    EARLY_TILES = TOK * 2 if first_stage else TILES
    EARLY = 2
    PER_GROUP = P // HD
    CLASSES = P // ROWS
    HALF = NU // 2
    QPG = PER_GROUP // QUAD
    QS = -1.0 / float(np.sqrt(HD))
    multiply = mask_kind != "added"
    mask_bufs = 1 if mask_kind == "shared" else 2
    small = HD < 32
    LAG, PROBS = (5, 8) if small else (3, 4)
    SUM_LAG = 2 if small else 1
    MASK_SLOT = 7
    TAIL = LAG + 3

    def sb(n, shape, dt=F32):
        return ctx.enter_context(nc.sbuf_tensor(f"{name}_{n}", shape, dt))

    q_w, k_w, v_w, o_w = weights
    q_b, k_b, v_b, o_b = biases
    cols = {"q": 0, "k": D, "o": 2 * D, "v": 3 * D}
    NC = 3 * D + KVD
    w_hi, w_lo = sb("w_hi", [P, KT, NC], F32R), sb("w_lo", [P, KT, NC], F32R)
    xn = sb("xn", [P, TOK, D])
    xt_hi, xt_lo = sb("xt_hi", [P, KT, TOKENS], F32R), sb("xt_lo", [P, KT, TOKENS], F32R)
    part_slots = 4 if small else 2
    part_hi, part_lo = (sb(n, [P, part_slots, 2, TOKENS], F32R) for n in ("part_hi", "part_lo"))
    q_stack, k_stack = (sb(n, [K, D // ROWS, TOKENS], F32R) for n in ("q_stack", "k_stack"))
    value = sb("value", [P, 2, TOK, kv_heads, 3 * HD]) if small else sb("value", [P, 2, TOK, D])
    masks = sb("masks", [P, mask_bufs, TOK, TOKENS])
    offset = sb("offset", [P, mask_bufs, TOK, TOKENS]) if multiply else masks
    prob = sb("prob", [P, PROBS, TOK, TOKENS])
    neg_max, sums, inv = (sb(n, [P, PROBS, TOK]) for n in ("neg_max", "sums", "inv"))
    prob_t = sb("prob_t", [P, 2 * QUAD, TOK, TOKENS])
    ring = prob_t[:, :, :, :].rearrange("p s t n -> p s (t n)")
    ctx_hi, ctx_lo = sb("ctx_hi", [P, GROUPS, TOKENS], F32R), sb("ctx_lo", [P, GROUPS, TOKENS], F32R)
    q_bias, k_bias = sb("q_bias", [P, GROUPS]), sb("k_bias", [P, GROUPS])
    v_bias, o_bias = sb("v_bias", [P, KVD]), sb("o_bias", [P, D])
    if norm:
        n_scale, n_bias = sb("n_scale", [P, D]), sb("n_bias", [P, D])

    score_bank, pt_bank = banks[0:2], banks[2:4]
    ctx_bank, proj_bank = [banks[4], banks[7]], banks[5:7]

    def out_bank(t):
        return proj_bank[(out_at + t) % 2][:, :]


    w_in = [ctx.enter_context(nc.semaphore(f"{name}_w_in{i}")) for i in range(STAGED)]
    enc_loaded = [ctx.enter_context(nc.semaphore(f"{name}_enc_loaded{t}")) for t in range(TOK)]
    stacked = {}
    s = semaphores(nc, ctx, name, """
        const_in norm_in w_high w_split x_first x_in neg_bias value_zero stats_in std_in rstd_in
        x_stats centred normed mask_loaded offset_in
        proj_done high_done proj_free scores_done masked k_bias_zero weight_zero maxed exp_done inv_done prob_done
        turned pt_even pt_odd pv_done ctx_high ctx_split out_done x_biased out_added stats_done
        sp_passed dve_passed""", w_in=w_in, enc_loaded=enc_loaded, stacked=stacked)

    if small:
        table = [("turn_x", 0, 3, 3, None), ("turn_x", 1, 4, 4, None), ("q", 0, 5, 7, 0), ("q", 1, 9, 11, 1),
                 ("turn_enc", 0, 12, 12, None), ("turn_enc", 1, 13, 13, None), ("k", 0, 19, 21, 2),
                 ("k", 1, 23, 25, 3), ("v", 0, 27, 28, None), ("v", 1, 30, 31, None)]
        out_slots, out_at, ctx_slots = (14, 15, 16, 17), 6, (19, 23, 31, 39)
    elif enc is not None:
        table = [("turn_x", 0, 3, 3, None), ("turn_x", 1, 4, 4, None), ("q", 0, 5, 6, 0), ("q", 1, 6, 7, 1),
                 ("turn_enc", 0, 8, 8, None), ("turn_enc", 1, 9, 9, None), ("k", 0, 10, 11, 0),
                 ("k", 1, 14, 15, 0), ("v", 0, 16, 17, None), ("v", 1, 17, 18, None)]
        out_slots, out_at, ctx_slots = (11, 12, 12, 13), 7, (14, 15, 17, 21)
    else:
        table = [("turn_x", 0, 3, 3, None), ("turn_x", 1, 4, 4, None), ("k", 0, 5, 6, 0), ("q", 0, 7, 8, 1),
                 ("k", 1, 12, 13, 0), ("q", 1, 14, 15, 1), ("v", 0, 16, 17, None), ("v", 1, 17, 18, None)]
        out_slots, out_at, ctx_slots = (9, 10, 11, 12), 4, (13, 14, 17, 21)
    uses = [u[:2] for u in table]
    halves = [u[2:4] for u in table]
    part_slot = {u[:2]: u[4] for u in table if u[4] is not None}
    NP = len(uses)
    left_at = [u[3] + (0 if "turn" in u[0] else 1) for u in table]
    assert all(a <= b for a, b in zip(left_at, left_at[1:])) and left_at[-1] <= left_at[0] + NU
    assert NP % 2 == 0
    index = {u: j for j, u in enumerate(uses)}
    highs = [u for u in uses if u[0] != "v"]
    NH = len(highs)
    parts = [u for u in uses if u[0] in "qk"]
    order = sorted(parts, key=lambda u: (u[1], index[u]))
    stacked.update({u: [ctx.enter_context(nc.semaphore(f"{name}_stacked_{u[0]}{u[1]}_{r}")) for r in range(CLASSES)]
                    for u in parts})
    N_DMA = 3
    N_CONST = 7 if small else 4

    def in_slot(t, slot, b, attend, finish):
        if slot == t and attend:
            return [b]
        if slot == t + NU and finish:
            return [prv(b)]
        return []

    def halves_at(t, b, project, attend):
        late = [(j, half, b) for j in range(NP) for half in range(2) if halves[j][half] == t + NU and attend]
        return late + [(j, half, nxt(b)) for j in range(NP) for half in range(2) if halves[j][half] == t and project]

    def evacuated_at(t, b, project, attend):
        late = [(j, b) for j in range(NP) if left_at[j] == t + NU and attend]
        return late + [(j, nxt(b)) for j in range(NP) if left_at[j] == t and project]

    def unit_at(t, lag, b, attend, finish):
        if t >= lag:
            return [(t - lag, b)] if attend else []
        return [(t - lag + NU, prv(b))] if finish else []

    def head_of(u):
        if not small:
            return u
        g, r = divmod(u, PER_GROUP)
        return g * PER_GROUP + 2 * (r % QUAD) + r // QUAD

    key_order = list(dict.fromkeys(u[0] for u in uses if u[0] in "qkv")) + ["o"]
    w_of = {"q": q_w, "k": k_w, "v": v_w, "o": o_w}
    chunks, chunk_end, chunk_start = [], {}, {}
    for key in key_order:
        chunk_start[key] = len(chunks)
        if small and key == "k":
            for k in range(KT):
                views = [part[:, k, D:2 * D].rearrange("p (g c) -> p g c", g=kv_heads) for part in (w_hi, w_lo)]
                for c in (0, 3 * HD):
                    chunks.append((k_w[k * P:(k + 1) * P, :], views[0][:, :, c:c + HD], views[1][:, :, c:c + HD], None))
        else:
            chunks += list(chunks_of(w_of[key], w_hi, w_lo, D, cols[key], QS if key == "q" else None))
        chunk_end[key] = len(chunks)
    split_before = {0: key_order[:1]}
    for key, next_key in zip(key_order, key_order[1:]):
        split_before.setdefault(index[(key, 0)], []).append(next_key)

    def w_part(key, k, a, b):
        c = cols[key]
        return w_hi[:, k, c + a:c + b], w_lo[:, k, c + a:c + b]

    block = ctx.enter_context(nc.Block())

    @block.sync
    def _(sp):
        small_in = [(q_bias[:, :], q_b.rearrange("(j p) -> p j", p=P)),
                    (v_bias[:, :], row_of(v_b, KVD)), (o_bias[:, :], row_of(o_b, D))]
        if small:
            sp.wait_ge(s.k_bias_zero, 1)
            for half in range(2):
                for c in (0, 3 * HD):
                    small_in.append((k_bias[64 * half + c:64 * half + c + HD, :],
                                     k_b.rearrange("(j g d) -> g d j", g=2, d=HD)[half]))
        else:
            small_in.append((k_bias[:, :], k_b.rearrange("(j p) -> p j", p=P)))
        if norm:
            for dst, src in ((n_scale, norm[0]), (n_bias, norm[1])):
                sp.dma_start(dst[:, :], row_of(src, D)).then_inc(s.norm_in, 16)

        def load_x(b):
            sp.dma_start(x[:, TOK * b:TOK * (b + 1), :], shared["x_dram"][b].rearrange("(t p) d -> p t d", p=P)
                         ).then_inc(s.x_first if b < EARLY else s.x_in, 16)

        if first_stage:
            for b in range(EARLY):
                load_x(b)
        load_chunks(sp, chunks, ring, s, 0, chunk_end[key_order[0]])
        for dst, src in small_in:
            sp.dma_start(dst, src, allow_slow_non_contiguous=True).then_inc(s.const_in, 16)

        def load_enc(b, t):
            rows = enc.rearrange("b (t p) d -> (b t) p d", p=P)
            n = at(b, TOK, t)
            src = rows[n] if isinstance(n, int) else rows[bass.ds(n, 1)].rearrange("a p d -> (a p) d")
            passed(sp, s.proj_done, at(b, NP, index[("turn_x", t)] + 1), s.sp_passed)
            sp.dma_start(xn[:, t, :], src).then_inc(s.enc_loaded[t], 16)

        def load_mask(b):
            n = at(b, 1)
            src = mask[0:1] if mask_kind == "shared" else mask[bass.ds(n, 1)] if not isinstance(n, int) else mask[n:n + 1]
            sp.dma_start(masks[:, b[1] % mask_bufs, :, :],
                         src.rearrange("a b (t p) n -> p (a b t) n", p=P)).then_inc(s.mask_loaded, 16)

        def stack(u, p):
            passed(sp, s.proj_free, at(p, NP, index[u] + 1), s.sp_passed)
            passed(sp, s.scores_done, at(prv(p), NU, (u[1] + 1) * HALF), s.sp_passed)
            stack_of = q_stack if u[0] == "q" else k_stack
            for r in range(CLASSES):
                for part in range(3):
                    low = part == (1 if u[0] == "q" else 2)
                    src = (part_lo if low else part_hi)[r * ROWS:(r + 1) * ROWS, part_slot[u], :, :]
                    g = 2 * CLASSES * u[1] + r
                    dst = stack_of[part * ROWS:(part + 1) * ROWS, g:g + CLASSES + 1:CLASSES, :]
                    sp.dma_start(dst.bitcast(F32), src.bitcast(F32)).then_inc(s.stacked[u][r], 16)

        def step(b, attend, project, finish):
            if not project:
                return
            p = nxt(b)
            if not attend:
                load_mask(p)
                load_chunks(sp, chunks, ring, s, chunk_end[key_order[0]], chunk_end[key_order[1]])
                if first_stage:
                    for n in range(EARLY, BATCHES):
                        load_x(n)
                if enc is not None:
                    for t in range(TOK):
                        load_enc(p, t)
                load_chunks(sp, chunks, ring, s, chunk_end[key_order[1]], None)
                for u in order:
                    stack(u, p)
                return
            if mask_kind != "shared":
                passed(sp, s.maxed, at(b, NU, 0), s.sp_passed)
                load_mask(p)
            if enc is not None:
                for t in range(TOK):
                    load_enc(p, t)
            for u in order:
                stack(u, p)

        over_batches(sp, step)

    @block.gpsimd
    def _(pool):
        if first_stage:
            nc.gpsimd.memset(ident[:, :], 0.0).then_inc(shared["ident_in"], 1)
            pool.wait_ge(shared["ident_in"], 1)
            nc.gpsimd.affine_select(out=ident[:, :], in_=ident[:, :], compare_op=ALU.not_equal, fill=1.0,
                                    base=0, pattern=[[-1, P]], channel_multiplier=1).then_inc(shared["ident_in"], 1)
        if small:
            nc.gpsimd.memset(k_bias[:, :], 0.0).then_inc(s.k_bias_zero, 1)
            nc.gpsimd.memset(w_hi[:, :, D:2 * D].bitcast(F32), 0.0).then_inc(s.weight_zero, 1)
            nc.gpsimd.memset(w_lo[:, :, D:2 * D].bitcast(F32), 0.0).then_inc(s.weight_zero, 1)
            nc.gpsimd.memset(value[:, :, :, :, :], 0.0).then_inc(s.value_zero, 1)
        pool.wait_ge(s.const_in, 16 * N_CONST)
        nc.gpsimd.tensor_scalar(q_bias[:, :], q_bias[:, :], QS, None, ALU.mult).then_inc(s.neg_bias, 1)

        def bias_x(b):
            wait(pool, s.normed, at(b, TOK, TOK))
            for t in range(TOK):
                tile = x[:, bass.ds(at(b, TOK, t), 1), :] if not isinstance(at(b, 1), int) else x[:, at(b, TOK, t):at(b, TOK, t) + 1, :]
                nc.gpsimd.tensor_tensor(tile, tile, o_bias[:, :].rearrange("p (a d) -> p a d", a=1),
                                        ALU.add).then_inc(s.x_biased, 1)

        def step(b, attend, project, finish):
            for t in range(NU if attend else SUM_LAG):
                for u, ub in unit_at(t, SUM_LAG, b, attend, finish):
                    pool.wait_ge(s.inv_done, at(ub, NU, u + 1))
                    pr = prob[:, u % PROBS, :, :]
                    nc.gpsimd.tensor_tensor(pr, pr, inv[:, u % PROBS, :].rearrange("p (t a) -> p t a", a=1)
                                            .broadcast_to([P, TOK, TOKENS]), ALU.mult).then_inc(s.prob_done, 1)
                if t == 8:
                    bias_x(b)

        over_batches(pool, step)

    @block.scalar
    def _(act):
        def roots(start, end, n):
            act.wait_ge(s.stats_in, n)
            nc.scalar.activation(rstd[:, start:end], rstd[:, start:end], ACT.Sqrt).then_inc(s.std_in, 1)

        if small:
            act.wait_ge(s.weight_zero, 2)
        if norm:
            roots(0, EARLY_TILES, 1)

        def high(j, p):
            u = uses[j]
            bank = proj_bank[j % 2]
            act.wait_ge(s.proj_done, at(p, NP, j + 1))
            if u[0] in ("turn_x", "turn_enc"):
                nc.scalar.activation(xt_hi[:, :, u[1] * P:(u[1] + 1) * P], bank[:, :].rearrange("p (k t) -> p k t", k=KT),
                                     ACT.Copy).then_inc(s.high_done, 1)
                return
            slot = part_slot[u]
            same = [v for v in parts if part_slot[v] == slot]
            v = same[same.index(u) - 1]
            for r in range(CLASSES):
                wait(act, s.stacked[v][r], at(p if index[v] < index[u] else prv(p), 16 * N_DMA, 16 * N_DMA))
            bias = q_bias if u[0] == "q" else k_bias
            if isinstance(p[0], int) and p == (0, 0):
                act.wait_ge(s.neg_bias, 1)
            for m in range(2):
                ins = nc.scalar.activation(part_hi[:, slot, m, :], bank[:, m * TOKENS:(m + 1) * TOKENS], ACT.Identity,
                                           bias=bias[:, 2 * u[1] + m:2 * u[1] + m + 1])
            ins.then_inc(s.high_done, 1)

        def evacuate(u, b):
            act.wait_ge(s.turned, at(b, NU, u + 1))
            if u % QUAD < 2:
                wait(act, s.pv_done, at(b, NQ, u // QUAD - 1))
            nc.scalar.activation(prob_t[:, u % (2 * QUAD), :, :].rearrange("p t n -> p (t n)"), pt_bank[u % 2][:, :],
                                 ACT.Copy).then_inc(s.pt_odd if u % 2 else s.pt_even, 1)

        def exponentials(u, b):
            act.wait_ge(s.maxed, at(b, NU, u + 1))
            for h in range(TOK):
                pr = prob[:, u % PROBS, h, :]
                ins = nc.scalar.activation(pr, pr, ACT.Exp, bias=neg_max[:, u % PROBS, h:h + 1], scale=-1.0,
                                           accum_out=sums[:, u % PROBS, h:h + 1])
            ins.then_inc(s.exp_done, 1)

        def context_high(g, b):
            act.wait_ge(s.pv_done, at(b, NQ, (g + 1) * QPG))
            wait(act, s.out_done, at(b, TOK))
            nc.scalar.activation(ctx_hi[:, g, :], ctx_bank[g % 2][:, 0:TOKENS], ACT.Copy).then_inc(s.ctx_high, 1)

        def step(b, attend, project, finish):
            if not attend and project:
                for j in range(NP):
                    for key in split_before.get(j, []):
                        high_chunks(nc, act, chunks, ring, s, chunk_start[key], chunk_end[key])
                    if uses[j] in highs and left_at[j] < NU:
                        high(j, nxt(b))
                return
            for t in range(NU if attend else TAIL):
                for u, ub in unit_at(t, LAG, b, attend, finish):
                    if not small or u % 2 == 0:
                        evacuate(u, ub)
                for j, p in evacuated_at(t, b, project, attend):
                    if uses[j] in highs:
                        high(j, p)
                for g in range(GROUPS):
                    for gb in in_slot(t, ctx_slots[g], b, attend, finish):
                        context_high(g, gb)
                if attend:
                    exponentials(t, b)
                if first_stage and attend and not finish and t == NU - 1:
                    roots(EARLY_TILES, TILES, 2)

        over_batches(act, step)

    @block.tensor
    def _(pe):
        if first_stage:
            pe.wait_ge(shared["ident_in"], 2)

        def project_use(j, half, p):
            u = uses[j]
            bank = proj_bank[j % 2]
            if half == 0:
                wait(pe, s.proj_free, at(p, NP, j - 1))
                if out_at <= j < out_at + TOK:
                    wait(pe, s.out_added, at(prv(prv(p)), TOK, j - out_at + 1))
            if u[0] in ("turn_x", "turn_enc"):
                if half == 1:
                    return
                t = u[1]
                if u[0] == "turn_x":
                    pe.wait_ge(s.normed, at(p, TOK, t + 1))
                    src = xn[:, t, :]
                else:
                    pe.wait_ge(s.enc_loaded[t], at(p, 16, 16))
                    src = xn[:, t, :]
                for k in range(KT):
                    ins = nc.tensor.transpose(bank[:, k * P:(k + 1) * P], src[:, k * P:(k + 1) * P], ident[:, :])
                ins.then_inc(s.proj_done, 1)
                return
            if half == 0:
                turned = index[("turn_enc" if enc is not None and u[0] in "kv" else "turn_x", 1)]
                pe.wait_ge(s.proj_free, at(p, NP, turned + 1))
                if isinstance(p[0], int) and p == (0, 0):
                    pe.wait_ge(s.w_split, chunk_end[u[0]])
            if u[0] == "v":
                for k in range(half * KT // 2, (half + 1) * KT // 2):
                    rows = xt_hi[:, k, u[1] * P:(u[1] + 1) * P], xt_lo[:, k, u[1] * P:(u[1] + 1) * P]
                    ins = passes(nc, bank[:, 0:KVD], rows, w_part("v", k, 0, KVD), k == 0, k == KT - 1)
            else:
                c = (2 * u[1] + half) * P
                for k in range(KT):
                    ins = passes(nc, bank[:, half * TOKENS:(half + 1) * TOKENS], w_part(u[0], k, c, c + P),
                                 (xt_hi[:, k, :], xt_lo[:, k, :]), k == 0, k == KT - 1)
            if half == 1:
                ins.then_inc(s.proj_done, 1)

        def scores(u, b):
            h = head_of(u)
            wait(pe, s.masked if multiply else s.maxed, at(b, NU, u - 1))
            if u % HALF < CLASSES:
                assert h * HD // ROWS % CLASSES == u % CLASSES
                for key in "qk":
                    pe.wait_ge(s.stacked[(key, u // HALF)][u % CLASSES], at(b, 16 * N_DMA, 16 * N_DMA))
            q_group = h * HD // ROWS
            k_group = h // REP * 2 + h % 2 if small else h
            for t in range(TOK):
                ins = nc.tensor.matmul(score_bank[u % 2][:, t * TOKENS:(t + 1) * TOKENS],
                                       q_stack[:, q_group, t * P:(t + 1) * P], k_stack[:, k_group, :],
                                       start=True, stop=True)
            ins.then_inc(s.scores_done, 1)

        def turn(u, b):
            pe.wait_ge(s.prob_done, at(b, NU, u + 1))
            wait(pe, s.pt_odd if u % 2 else s.pt_even, at(b, NU // 2, u // 2))
            for kt in range(TOK):
                for t in range(TOK):
                    c = kt * TOKENS + t * P
                    ins = nc.tensor.transpose(pt_bank[u % 2][:, c:c + P], prob[:, u % PROBS, t, kt * P:(kt + 1) * P], ident[:, :])
            ins.then_inc(s.turned, 1)

        def times_values(q, b):
            g = q // QPG
            pe.wait_ge(s.pt_even, at(b, NU // 2, 2 * (q + 1)))
            pe.wait_ge(s.pt_odd, at(b, NU // 2, 2 * (q + 1)))
            if q == 0:
                last_v = max(index[u] for u in uses if u[0] == "v")
                pe.wait_ge(s.proj_free, at(b, NP, last_v + 1))
            if q % QPG == 0:
                wait(pe, s.ctx_split, at(b, GROUPS, g - 1))
            first, last = q % QPG == 0, q % QPG == QPG - 1
            for kt in range(TOK):
                for i in range(QUAD):
                    u = q * QUAD + i
                    h = head_of(u)
                    if small:
                        c = HD * (1 - q % 2)
                        v = value[:, b[1] % 2, kt, h // REP, c:c + 2 * HD]
                    else:
                        v = value[:, b[1] % 2, kt, h * HD:(h + 1) * HD]
                    ins = nc.tensor.matmul(ctx_bank[g % 2][32 * i:32 * i + 32, 0:TOKENS], v, prob_t[:, u % (2 * QUAD), kt, :],
                                           start=first and kt == 0, stop=last and kt == TOK - 1)
            ins.then_inc(s.pv_done, 1)

        def project_out(t, half, b, p, projecting):
            if half == 0:
                if t == 0:
                    pe.wait_ge(s.ctx_split, at(b, GROUPS, GROUPS))
                    if not projecting:
                        pe.wait_ge(s.proj_free, NP * BATCHES)
                if projecting:
                    pe.wait_ge(s.proj_free, at(p, NP, out_at - 1 + t))
                else:
                    wait(pe, s.out_added, at(b, TOK, t + 1 - TOK))
            for k in range(half * KT // 2, (half + 1) * KT // 2):
                rows = ctx_hi[:, k, t * P:(t + 1) * P], ctx_lo[:, k, t * P:(t + 1) * P]
                ins = passes(nc, out_bank(t), rows, w_part("o", k, 0, D), k == 0, k == KT - 1)
            if half == 1:
                ins.then_inc(s.out_done, 1)

        def step(b, attend, project, finish):
            if not attend and project:
                for j in range(NP):
                    for half in range(2):
                        if halves[j][half] < NU:
                            project_use(j, half, nxt(b))
                pe.wait_ge(s.w_split, len(chunks))
                scores(0, nxt(b))
                return
            for t in range(NU if attend else TAIL):
                for u, ub in unit_at(t, LAG, b, attend, finish):
                    turn(u, ub)
                for q in range(NQ):
                    for qb in in_slot(t, LAG + QUAD * (q + 1) + 1, b, attend, finish):
                        times_values(q, qb)
                if attend and t + 1 < NU:
                    scores(t + 1, b)
                elif attend and project:
                    scores(0, nxt(b))
                for i, slot in enumerate(out_slots):
                    if slot == t and finish and attend:
                        project_out(i // 2, i % 2, prv(b), nxt(b), project)
                for j, half, p in halves_at(t, b, project, attend):
                    project_use(j, half, p)
            if not attend:
                for i in range(2 * TOK):
                    project_out(i // 2, i % 2, prv(b), None, False)

        over_batches(pe, step)

    @block.vector
    def _(dve):
        def first_stats(start, end):
            for i in range(start, end):
                nc.vector.bn_stats(stats[:, i, :], x[:, i, :]).then_inc(s.x_stats, 1)

        def inverse_roots(start, end, n):
            dve.wait_ge(s.std_in, n)
            nc.vector.reciprocal(rstd[:, start:end], rstd[:, start:end]).then_inc(s.rstd_in, 1)
            dve.wait_ge(s.rstd_in, n)

        if norm:
            if first_stage:
                dve.wait_ge(s.x_first, 16 * EARLY)
                first_stats(0, TOK * EARLY)
                dve.wait_ge(s.x_stats, TOK * EARLY)
            aggregate(nc, shared, 1e-5, 0, EARLY_TILES).then_inc(s.stats_in, 1)
            inverse_roots(0, EARLY_TILES, 1)
        if small:
            dve.wait_ge(s.value_zero, 1)

        def tile_of(arr, n):
            return arr[:, n:n + 1] if isinstance(n, int) else arr[:, bass.ds(n, 1)]

        def normalise(t, p):
            last = index[("turn_x" if enc is None else "turn_enc", 1)]
            wait(dve, s.proj_done, at(prv(p), NP, last + 1))
            n = at(p, TOK, t)
            src = x[:, n:n + 1, :] if isinstance(n, int) else x[:, bass.ds(n, 1), :]
            dst = xn[:, t:t + 1, :]
            if norm:
                nc.vector.scalar_tensor_tensor(out=dst, in0=src, scalar=tile_of(mean, n), in1=n_scale[:, :].rearrange("p (a d) -> p a d", a=1),
                                               op0=ALU.subtract, op1=ALU.mult).then_inc(s.centred, 1)
            else:
                nc.vector.tensor_copy(dst, src).then_inc(s.normed, 1)

        def finish_normalise(t, p):
            dve.wait_ge(s.centred, at(p, TOK, t + 1))
            dst = xn[:, t:t + 1, :]
            nc.vector.scalar_tensor_tensor(out=dst, in0=dst, scalar=tile_of(rstd, at(p, TOK, t)),
                                           in1=n_bias[:, :].rearrange("p (a d) -> p a d", a=1),
                                           op0=ALU.mult, op1=ALU.add).then_inc(s.normed, 1)

        def offsets(p):
            buf = p[1] % mask_bufs
            dve.wait_ge(s.mask_loaded, at(p, 16, 16) if mask_kind != "shared" else 16)
            dve.sem_inc(s.dve_passed, 1)
            a, c = (1.0, -10000.0) if multiply else (0.0, -1.0)
            nc.vector.tensor_scalar(offset[:, buf, :, :], masks[:, buf, :, :], a, c, ALU.subtract,
                                    ALU.mult).then_inc(s.offset_in, 1)

        def low(j, p):
            u = uses[j]
            bank = proj_bank[j % 2]
            if u[0] == "v":
                dve.wait_ge(s.proj_done, at(p, NP, j + 1))
                if small:
                    ins = nc.vector.tensor_tensor(value[:, p[1] % 2, u[1], :, HD:2 * HD],
                                                  bank[:, 0:KVD].rearrange("p (h d) -> p h d", d=HD),
                                                  v_bias[:, :].rearrange("p (h d) -> p h d", d=HD), ALU.add)
                else:
                    ins = nc.vector.tensor_tensor(value[:, p[1] % 2, u[1], :], bank[:, :], v_bias[:, :], ALU.add)
                ins.then_inc(s.proj_free, 1)
                return
            dve.wait_ge(s.high_done, at(p, NH, highs.index(u) + 1))
            if u[0] in ("turn_x", "turn_enc"):
                c = slice(u[1] * P, (u[1] + 1) * P)
                nc.vector.tensor_tensor(xt_lo[:, :, c], bank[:, :].rearrange("p (k t) -> p k t", k=KT),
                                        xt_hi[:, :, c].bitcast(F32), ALU.subtract).then_inc(s.proj_free, 1)
                return
            slot = part_slot[u]
            bias = q_bias if u[0] == "q" else k_bias
            for m in range(2):
                ins = nc.vector.scalar_tensor_tensor(out=part_lo[:, slot, m, :], in0=bank[:, m * TOKENS:(m + 1) * TOKENS],
                                                     scalar=bias[:, 2 * u[1] + m:2 * u[1] + m + 1],
                                                     in1=part_hi[:, slot, m, :].bitcast(F32), op0=ALU.add, op1=ALU.subtract)
            ins.then_inc(s.proj_free, 1)

        def add_out(t, b):
            dve.wait_ge(s.out_done, at(b, TOK, t + 1))
            dve.wait_ge(s.x_biased, at(b, TOK, t + 1))
            n = at(b, TOK, t)
            tile = x[:, n:n + 1, :] if isinstance(n, int) else x[:, bass.ds(n, 1), :]
            nc.vector.tensor_tensor(tile, out_bank(t).rearrange("p (a d) -> p a d", a=1), tile,
                                    ALU.add).then_inc(s.out_added, 1)

        def take_stats(t, b):
            dve.wait_ge(s.out_added, at(b, TOK, t + 1))
            n = at(b, TOK, t)
            tile = x[:, n, :] if isinstance(n, int) else x[:, bass.ds(n, 1), :]
            st = stats[:, n, :] if isinstance(n, int) else stats[:, bass.ds(n, 1), :]
            nc.vector.bn_stats(st, tile).then_inc(s.stats_done, 1)

        def reciprocals(u, b):
            dve.wait_ge(s.exp_done, at(b, NU, u + 1))
            nc.vector.reciprocal(inv[:, u % PROBS, :], sums[:, u % PROBS, :]).then_inc(s.inv_done, 1)

        def mask_and_max(t, b):
            buf = b[1] % mask_bufs
            if multiply:
                dve.wait_ge(s.masked, at(b, NU, t + 1))
            dve.sem_inc(s.dve_passed, 1)
            for h in range(TOK):
                src = prob[:, t % PROBS, h, :] if multiply else score_bank[t % 2][:, h * TOKENS:(h + 1) * TOKENS]
                ins = nc.vector.tensor_tensor_reduce(out=prob[:, t % PROBS, h, :], in0=src, in1=offset[:, buf, h, :],
                                                     scale=1.0, scalar=BIG, op0=ALU.add, op1=ALU.min,
                                                     accum_out=neg_max[:, t % PROBS, h:h + 1])
            ins.then_inc(s.maxed, 1)

        def evacuate(u, b):
            dve.wait_ge(s.turned, at(b, NU, u + 1))
            if u % QUAD < 2:
                wait(dve, s.pv_done, at(b, NQ, u // QUAD - 1))
            nc.vector.tensor_copy(prob_t[:, u % (2 * QUAD), :, :].rearrange("p t n -> p (t n)"),
                                  pt_bank[1][:, :]).then_inc(s.pt_odd, 1)

        def context_low(g, b):
            dve.wait_ge(s.ctx_high, at(b, GROUPS, g + 1))
            nc.vector.tensor_tensor(ctx_lo[:, g, :], ctx_bank[g % 2][:, 0:TOKENS], ctx_hi[:, g, :].bitcast(F32),
                                    ALU.subtract).then_inc(s.ctx_split, 1)

        def step(b, attend, project, finish):
            if not attend and project:
                if norm:
                    dve.wait_ge(s.norm_in, 32)
                for t in range(TOK):
                    normalise(t, nxt(b))
                if norm:
                    for t in range(TOK):
                        finish_normalise(t, nxt(b))
                for j in range(NP):
                    if j == TOK:
                        dve.wait_ge(s.const_in, 16 * N_CONST)
                        dve.wait_ge(s.neg_bias, 1)
                    for key in split_before.get(j, []):
                        low_chunks(nc, dve, chunks, ring, s, chunk_start[key], chunk_end[key])
                    if left_at[j] < NU:
                        low(j, nxt(b))
                offsets(nxt(b))
                return
            for t in range(NU if attend else TAIL):
                if attend:
                    dve.wait_ge(s.scores_done, at(b, NU, t + 1))
                    wait(dve, s.turned, at(b, NU, t + 1 - PROBS))
                    if t == 0:
                        dve.wait_ge(s.offset_in, 1 if mask_kind == "shared" else at(b, 1, 1))
                    if multiply:
                        nc.vector.tensor_tensor(prob[:, t % PROBS, :, :].rearrange("p t n -> p (t n)"), score_bank[t % 2][:, :],
                                                masks[:, b[1] % mask_bufs, :, :].rearrange("p t n -> p (t n)"),
                                                ALU.mult).then_inc(s.masked, 1)
                if attend:
                    mask_and_max(t, b)
                for u, ub in unit_at(t, SUM_LAG, b, attend, finish):
                    reciprocals(u, ub)
                for u, ub in unit_at(t, LAG, b, attend, finish):
                    if small and u % 2 == 1:
                        evacuate(u, ub)
                if project and attend and t < TOK:
                    normalise(t, nxt(b))
                if norm and project and attend and 1 <= t <= TOK:
                    finish_normalise(t - 1, nxt(b))
                if project and attend and t == MASK_SLOT and mask_kind != "shared":
                    offsets(nxt(b))
                if finish and attend:
                    for i in range(TOK):
                        if t == out_slots[2 * i + 1] + 1:
                            add_out(i, prv(b))
                        if t == out_slots[2 * i + 1] + 2:
                            take_stats(i, prv(b))
                for j, p in evacuated_at(t, b, project, attend):
                    low(j, p)
                for g in range(GROUPS):
                    for gb in in_slot(t, ctx_slots[g], b, attend, finish):
                        context_low(g, gb)
                if first_stage and attend and not finish:
                    i = TOK * EARLY + 2 * (t - 8)
                    if 8 <= t and i < TILES:
                        dve.wait_ge(s.x_in, 16 * (BATCHES - EARLY))
                        first_stats(i, i + 2)
                    if t == NU - 2:
                        dve.wait_ge(s.x_stats, TILES)
                        aggregate(nc, shared, 1e-5, EARLY_TILES, TILES).then_inc(s.stats_in, 1)
                    if t == NU - 1:
                        inverse_roots(EARLY_TILES, TILES, 2)
            if not attend:
                for t in range(TOK):
                    add_out(t, prv(b))
                for t in range(TOK):
                    take_stats(t, prv(b))

        over_batches(dve, step)


def aggregate(nc, shared, eps, start=0, end=TILES):
    stats, moments, mean, rstd = (shared[n] for n in ("stats", "moments", "mean", "rstd"))
    done = shared["moments_done"]
    for i in range(start, end):
        nc.vector.bn_aggr(moments[:, i, :], stats[:, i, :]).then_inc(done, 1)
    shared["n_moments"] += end - start
    nc.vector.wait_ge(done, shared["n_moments"])
    nc.vector.tensor_copy(mean[:, start:end], moments[:, start:end, 0])
    return nc.vector.tensor_scalar(rstd[:, start:end], moments[:, start:end, 1], eps, None, ALU.add)


def mlp_stage(nc, ctx, shared, w1, b1, w2, b2, norm):
    x, mean, rstd, stats, ident, banks = (shared[n] for n in ("x", "mean", "rstd", "stats", "ident", "banks"))
    F = w1.shape[1]
    FT = F // P
    PAIRS = FT // 2
    HELD = 4

    def sb(n, shape, dt=F32):
        return ctx.enter_context(nc.sbuf_tensor(f"mlp_{n}", shape, dt))

    w1_hi, w1_lo = sb("w1_hi", [P, KT, F], F32R), sb("w1_lo", [P, KT, F], F32R)
    w2_hi, w2_lo = sb("w2_hi", [P, FT, D], F32R), sb("w2_lo", [P, FT, D], F32R)
    xn = sb("xn", [P, TOK, D])
    xt_hi, xt_lo = sb("xt_hi", [P, KT, TOKENS], F32R), sb("xt_lo", [P, KT, TOKENS], F32R)
    ring = sb("ring", [P, MLP_STAGED, 2 * TOKENS])
    lin, act_in = ring[:, 0:2, :], ring[:, 2:4, :]
    hid_hi, hid_lo = sb("hid_hi", [P, HELD, 2 * TOKENS], F32R), sb("hid_lo", [P, HELD, 2 * TOKENS], F32R)
    b1_col, b2_row = sb("b1_col", [P, FT]), sb("b2_row", [P, D])
    n_scale, n_bias = sb("n_scale", [P, D]), sb("n_bias", [P, D])
    hid_bank, out_bank, turn_bank = banks[0:4], [banks[4], banks[7]], banks[5:7]
    s = semaphores(nc, ctx, "mlp", """
        const_in norm_in w_high w_split stats_in std_in rstd_in centred normed turned high_done turn_split
        hid_done lin_done poly_done inner_done tanh_done gelu_done hid_high hid_split part_done
        x_biased out_added stats_done""",
                   w_in=[ctx.enter_context(nc.semaphore(f"mlp_w_in{i}")) for i in range(MLP_STAGED)])
    chunks = [c for n in range(0, F, 512) for c in chunks_of(w1[:, n:n + 512], w1_hi, w1_lo, D, n)]
    chunks += list(chunks_of(w2, w2_hi, w2_lo, F, 0, 0.5))
    AHEAD = 3
    block = ctx.enter_context(nc.Block())

    def over(eng, step):
        step((0, -1), False, True)
        step((0, 0), True, True)
        with eng.Fori(0, BATCHES // 2 - 1) as r:
            step((r, 1), True, True)
            step((r, 2), True, True)
        step((BATCHES // 2 - 1, 1), True, False)

    @block.sync
    def _(sp):
        for dst, src in ((n_scale, norm[0]), (n_bias, norm[1])):
            sp.dma_start(dst[:, :], row_of(src, D)).then_inc(s.norm_in, 16)
        load_chunks(sp, chunks, ring, s, 0, KT)
        for dst, src in ((b1_col[:, :], b1.rearrange("(j p) -> p j", p=P)), (b2_row[:, :], row_of(b2, D))):
            sp.dma_start(dst, src, allow_slow_non_contiguous=True).then_inc(s.const_in, 16)
        load_chunks(sp, chunks, ring, s, KT, None)

    @block.gpsimd
    def _(pool):
        pool.wait_ge(s.const_in, 32)

        def step(b, work, prepare):
            p = nxt(b)
            if prepare:
                pool.wait_ge(s.normed, at(p, TOK, TOK))
                for t in range(TOK):
                    n = at(p, TOK, t)
                    tile = x[:, n:n + 1, :] if isinstance(n, int) else x[:, bass.ds(n, 1), :]
                    nc.gpsimd.tensor_tensor(tile, tile, b2_row[:, :].rearrange("p (a d) -> p a d", a=1),
                                            ALU.add).then_inc(s.x_biased, 1)

        over(pool, step)

    @block.scalar
    def _(act):
        act.wait_ge(s.stats_in, 1)
        nc.scalar.activation(rstd[:, :], rstd[:, :], ACT.Sqrt).then_inc(s.std_in, 1)
        act.wait_ge(s.const_in, 32)

        def turn_high(i, p):
            act.wait_ge(s.turned, at(p, 2, i + 1))
            nc.scalar.activation(xt_hi[:, 2 * i:2 * i + 2, :].rearrange("p k t -> p (k t)"), turn_bank[i][:, :],
                                 ACT.Copy).then_inc(s.high_done, 1)

        def tanh(n, b):
            act.wait_ge(s.inner_done, at(b, PAIRS, n + 1))
            nc.scalar.activation(act_in[:, n % 2, :], act_in[:, n % 2, :], ACT.Tanh).then_inc(s.tanh_done, 1)

        def step(b, work, prepare):
            p = nxt(b)
            if work:
                for n in range(PAIRS + 1):
                    if n < PAIRS:
                        act.wait_ge(s.hid_done, at(b, PAIRS, n + 1))
                        wait(act, s.hid_split, at(b, PAIRS, n - 1))
                        bank = hid_bank[n % 4]
                        for m in range(2):
                            c = slice(m * TOKENS, (m + 1) * TOKENS)
                            bias = b1_col[:, 2 * n + m:2 * n + m + 1]
                            nc.scalar.activation(lin[:, n % 2, c], bank[:, c], ACT.Identity, bias=bias)
                            ins = nc.scalar.activation(act_in[:, n % 2, c], bank[:, c], ACT.Square, bias=bias)
                        ins.then_inc(s.lin_done, 1)
                    if n >= 1:
                        tanh(n - 1, b)
            if not work:
                high_chunks(nc, act, chunks, ring, s, 0, KT)
            if prepare:
                for i in range(2):
                    turn_high(i, p)
            if not work:
                high_chunks(nc, act, chunks, ring, s, KT, None)
                act.wait_ge(s.w_split, len(chunks))

        over(act, step)

    @block.tensor
    def _(pe):
        def hidden(n, b):
            wait(pe, s.lin_done, at(b, PAIRS, n - 3))
            if n == 0:
                pe.wait_ge(s.turn_split, at(b, 2, 2))
            if isinstance(b[0], int) and b == (0, 0) and n % 2 == 0:
                pe.wait_ge(s.w_split, KT * (n // 2 + 1))
            for m in range(2):
                c = (2 * n + m) * P
                for k in range(KT):
                    ins = passes(nc, hid_bank[n % 4][:, m * TOKENS:(m + 1) * TOKENS],
                                 (w1_hi[:, k, c:c + P], w1_lo[:, k, c:c + P]), (xt_hi[:, k, :], xt_lo[:, k, :]),
                                 k == 0, k == KT - 1)
            ins.then_inc(s.hid_done, 1)

        def out_part(n, b):
            pe.wait_ge(s.hid_split, at(b, PAIRS, n + 1))
            if n == 0:
                wait(pe, s.out_added, at(b, TOK))
                pe.wait_ge(s.w_split, len(chunks))
            for t in range(TOK):
                for m in range(2):
                    k = 2 * n + m
                    c = m * TOKENS + t * P
                    ins = passes(nc, out_bank[t][:, :], (hid_hi[:, n % HELD, c:c + P], hid_lo[:, n % HELD, c:c + P]),
                                 (w2_hi[:, k, :], w2_lo[:, k, :]), k == 0, k == FT - 1)
            ins.then_inc(s.part_done, 1)

        def turn(i, p):
            wait(pe, s.turn_split, at(p, 2, i - 1))
            if i == 0:
                pe.wait_ge(s.normed, at(p, TOK, TOK))
            for kk in range(2):
                for t in range(TOK):
                    c, k = kk * TOKENS + t * P, 2 * i + kk
                    ins = nc.tensor.transpose(turn_bank[i][:, c:c + P], xn[:, t, k * P:(k + 1) * P], ident[:, :])
            ins.then_inc(s.turned, 1)

        def step(b, work, prepare):
            p = nxt(b)
            if work:
                for n in range(PAIRS):
                    hidden(n, b)
                    if n >= AHEAD:
                        out_part(n - AHEAD, b)
            if prepare:
                for i in range(2):
                    turn(i, p)
            if work:
                for n in range(PAIRS - AHEAD, PAIRS):
                    out_part(n, b)

        over(pe, step)

    @block.vector
    def _(dve):
        aggregate(nc, shared, 1e-5).then_inc(s.stats_in, 1)
        dve.wait_ge(s.std_in, 1)
        nc.vector.reciprocal(rstd[:, :], rstd[:, :]).then_inc(s.rstd_in, 1)
        dve.wait_ge(s.rstd_in, 1)
        dve.wait_ge(s.norm_in, 32)

        def polynomial(n, b):
            a = act_in[:, n % 2, :]
            dve.wait_ge(s.lin_done, at(b, PAIRS, n + 1))
            nc.vector.tensor_scalar(a, a, GELU_C * GELU_A, GELU_C, ALU.mult, ALU.add).then_inc(s.poly_done, 1)
            dve.wait_ge(s.poly_done, at(b, PAIRS, n + 1))
            nc.vector.tensor_tensor(a, a, lin[:, n % 2, :], ALU.mult).then_inc(s.inner_done, 1)

        def gelu(n, b):
            u = lin[:, n % 2, :]
            dve.wait_ge(s.tanh_done, at(b, PAIRS, n + 1))
            nc.vector.scalar_tensor_tensor(out=u, in0=act_in[:, n % 2, :], scalar=1.0, in1=u, op0=ALU.add,
                                           op1=ALU.mult).then_inc(s.gelu_done, 1)
            wait(dve, s.part_done, at(b, PAIRS, n + 1 - HELD))
            dve.wait_ge(s.gelu_done, at(b, PAIRS, n + 1))
            nc.vector.tensor_copy(hid_hi[:, n % HELD, :], u).then_inc(s.hid_high, 1)
            dve.wait_ge(s.hid_high, at(b, PAIRS, n + 1))
            nc.vector.tensor_tensor(hid_lo[:, n % HELD, :], u, hid_hi[:, n % HELD, :].bitcast(F32),
                                    ALU.subtract).then_inc(s.hid_split, 1)

        def tile_of(arr, n):
            return arr[:, n:n + 1] if isinstance(n, int) else arr[:, bass.ds(n, 1)]

        def normalise(t, p):
            wait(dve, s.turned, at(p, 2))
            n = at(p, TOK, t)
            src = x[:, n:n + 1, :] if isinstance(n, int) else x[:, bass.ds(n, 1), :]
            dst = xn[:, t:t + 1, :]
            nc.vector.scalar_tensor_tensor(out=dst, in0=src, scalar=tile_of(mean, n), in1=n_scale[:, :].rearrange("p (a d) -> p a d", a=1),
                                           op0=ALU.subtract, op1=ALU.mult).then_inc(s.centred, 1)
            dve.wait_ge(s.centred, at(p, TOK, t + 1))
            nc.vector.scalar_tensor_tensor(out=dst, in0=dst, scalar=tile_of(rstd, n),
                                           in1=n_bias[:, :].rearrange("p (a d) -> p a d", a=1),
                                           op0=ALU.mult, op1=ALU.add).then_inc(s.normed, 1)

        def step(b, work, prepare):
            p = nxt(b)
            if prepare:
                for t in range(TOK):
                    normalise(t, p)
            if not work:
                low_chunks(nc, dve, chunks, ring, s, 0, KT)
            if work:
                for n in range(PAIRS + 1):
                    if n < PAIRS:
                        polynomial(n, b)
                    if n >= 1:
                        gelu(n - 1, b)
            if prepare:
                for i in range(2):
                    dve.wait_ge(s.high_done, at(p, 2, i + 1))
                    nc.vector.tensor_tensor(xt_lo[:, 2 * i:2 * i + 2, :].rearrange("p k t -> p (k t)"), turn_bank[i][:, :],
                                            xt_hi[:, 2 * i:2 * i + 2, :].rearrange("p k t -> p (k t)").bitcast(F32),
                                            ALU.subtract).then_inc(s.turn_split, 1)
            if not work:
                low_chunks(nc, dve, chunks, ring, s, KT, None)
            if work:
                dve.wait_ge(s.part_done, at(b, PAIRS, PAIRS))
                dve.wait_ge(s.x_biased, at(b, TOK, TOK))
                for t in range(TOK):
                    n = at(b, TOK, t)
                    tile = x[:, n:n + 1, :] if isinstance(n, int) else x[:, bass.ds(n, 1), :]
                    nc.vector.tensor_tensor(tile, out_bank[t][:, :].rearrange("p (a d) -> p a d", a=1), tile,
                                            ALU.add).then_inc(s.out_added, 1)

        over(dve, step)


def last_norm(nc, ctx, shared, gamma, beta, out):
    x, mean, rstd = shared["x"], shared["mean"], shared["rstd"]
    scale = ctx.enter_context(nc.sbuf_tensor("last_scale", [P, D], F32))
    bias = ctx.enter_context(nc.sbuf_tensor("last_bias", [P, D], F32))
    shift = ctx.enter_context(nc.sbuf_tensor("last_shift", [P, TILES], F32))
    s = semaphores(nc, ctx, "last", """const_in stats_in std_in rstd_in shift_in centred dve_ready
        normed scaled pool_ready stored""")
    ON_POOL = range(2, TILES, 3)
    block = ctx.enter_context(nc.Block())

    @block.sync
    def _(sp):
        sp.dma_start(scale[:, :], row_of(gamma, D)).then_inc(s.const_in, 16)
        sp.dma_start(bias[:, :], row_of(beta, D)).then_inc(s.const_in, 16)
        for i in range(TILES):
            b, t = divmod(i, TOK)
            on_pool = len([n for n in ON_POOL if n <= i])
            if i in ON_POOL:
                sp.wait_ge(s.pool_ready, on_pool)
            else:
                sp.wait_ge(s.dve_ready, i + 1 - on_pool)
            sp.dma_start(out[b, t * P:(t + 1) * P, :], x[:, i, :]).then_inc(s.stored, 16)
        sp.wait_ge(s.stored, 16 * TILES)

    @block.scalar
    def _(act):
        act.wait_ge(s.stats_in, 1)
        nc.scalar.activation(rstd[:, :], rstd[:, :], ACT.Sqrt).then_inc(s.std_in, 1)
        act.wait_ge(s.shift_in, 1)
        for i in ON_POOL:
            nc.scalar.activation(x[:, i, :], x[:, i, :], ACT.Identity, bias=shift[:, i:i + 1],
                                 scale=rstd[:, i:i + 1]).then_inc(s.normed, 1)

    @block.vector
    def _(dve):
        aggregate(nc, shared, 1e-6).then_inc(s.stats_in, 1)
        dve.wait_ge(s.std_in, 1)
        nc.vector.reciprocal(rstd[:, :], rstd[:, :]).then_inc(s.rstd_in, 1)
        dve.wait_ge(s.rstd_in, 1)
        nc.vector.scalar_tensor_tensor(out=shift[:, :], in0=mean[:, :], scalar=-1.0, in1=rstd[:, :], op0=ALU.mult,
                                       op1=ALU.mult).then_inc(s.shift_in, 1)
        dve.wait_ge(s.const_in, 32)
        tiles = [i for i in range(TILES) if i not in ON_POOL]
        for n in range(len(tiles) + 1):
            if n < len(tiles):
                i = tiles[n]
                nc.vector.scalar_tensor_tensor(out=x[:, i, :], in0=x[:, i, :], scalar=mean[:, i:i + 1], in1=scale[:, :],
                                               op0=ALU.subtract, op1=ALU.mult).then_inc(s.centred, 1)
            if n >= 1:
                i = tiles[n - 1]
                dve.wait_ge(s.centred, n)
                nc.vector.scalar_tensor_tensor(out=x[:, i, :], in0=x[:, i, :], scalar=rstd[:, i:i + 1], in1=bias[:, :],
                                               op0=ALU.mult, op1=ALU.add).then_inc(s.dve_ready, 1)

    @block.gpsimd
    def _(pool):
        pool.wait_ge(s.const_in, 32)
        for n, i in enumerate(ON_POOL):
            pool.wait_ge(s.normed, n + 1)
            nc.gpsimd.tensor_tensor(x[:, i, :], x[:, i, :], scale[:, :], ALU.mult).then_inc(s.scaled, 1)
            pool.wait_ge(s.scaled, n + 1)
            nc.gpsimd.tensor_tensor(x[:, i, :], x[:, i, :], bias[:, :], ALU.add).then_inc(s.pool_ready, 1)


@contextmanager
def stage_of(nc):
    with ExitStack() as ctx:
        before = set(nc.free_semaphores)
        held = []
        with ExitStack() as inner:
            yield inner
            held = sorted(before - set(nc.free_semaphores))
        at_ = 0
        while at_ < len(held):
            end = at_
            while end + 1 < len(held) and held[end + 1] == held[end] + 1:
                end += 1
            nc.gpsimd.sem_clear(range(held[at_], held[end] + 1))
            at_ = end + 1
        nc.all_engine_barrier()


def build(nc, a, out):
    with ExitStack() as ctx:
        shared = {"x_dram": a["x"]}
        for n, shape in (("x", [P, TILES, D]), ("mean", [P, TILES]), ("rstd", [P, TILES]),
                         ("stats", [P, TILES, 6]), ("moments", [P, TILES, 2]), ("ident", [P, P])):
            shared[n] = ctx.enter_context(nc.sbuf_tensor(n, shape, F32))
        shared["banks"] = [ctx.enter_context(nc.psum_tensor(f"bank{i}", [P, 512], F32)) for i in range(8)]
        shared["ident_in"] = ctx.enter_context(nc.semaphore("ident_in"))
        shared["moments_done"] = ctx.enter_context(nc.semaphore("moments_done"))
        shared["n_moments"] = 0
        L0 = {k[len("L0_xattn_"):]: v for k, v in a.items() if k.startswith("L0_xattn_")}
        L1 = {k[len("L1_xattn_"):]: v for k, v in a.items() if k.startswith("L1_xattn_")}
        qkv, bqkv, kv, bkv = L0["w_qkv"], L0["b_qkv"], L0["w_kv"], L0["b_kv"]
        with stage_of(nc) as stage:
            attention_stage(nc, stage, "self", shared, out, q_src="x",
                            weights=(qkv[:, 0:D], qkv[:, D:2 * D], qkv[:, 2 * D:3 * D], L0["w_ao"]),
                            biases=(bqkv[0:D], bqkv[D:2 * D], bqkv[2 * D:3 * D], L0["b_ao"]),
                            norm=(L0["ln1_s"], L0["ln1_b"]), mask=a["mask_1x1xSxS2_fc1"], mask_kind="shared",
                            enc=None, heads=16, kv_heads=16, first_stage=True)
        with stage_of(nc) as stage:
            attention_stage(nc, stage, "cross", shared, out, q_src="x",
                            weights=(L0["w_q"], kv[:, 0:D], kv[:, D:2 * D], L0["w_co"]),
                            biases=(L0["b_q"], bkv[0:D], bkv[D:2 * D], L0["b_co"]),
                            norm=(L0["ln2_s"], L0["ln2_b"]), mask=a["mask_Bx1xSxS2_ff1"], mask_kind="batch",
                            enc=a["ctx_2048"], heads=16, kv_heads=16)
        with stage_of(nc) as stage:
            mlp_stage(nc, stage, shared, L0["w1"], L0["b1"], L0["w2"], L0["b2"], (L0["ln3_s"], L0["ln3_b"]))
        with stage_of(nc) as stage:
            attention_stage(nc, stage, "gqa", shared, out, q_src="x",
                            weights=(L1["Wq"], L1["Wk"], L1["Wv"], L1["Wo"]),
                            biases=(L1["bq"], L1["bk"], L1["bv"], L1["bo"]),
                            norm=None, mask=a["mask_Bx1xSxS2_ff0"], mask_kind="added",
                            enc=a["ctx_2048"], heads=32, kv_heads=8)
        with stage_of(nc) as stage:
            last_norm(nc, stage, shared, L1["gamma"], L1["beta"], out)


def kernel(**inputs):
    import numpy as _np
    import concourse.bacc as _bacc
    from concourse import mybir as _mybir
    from concourse.bass_utils import run_bass_kernel_spmd as _run

    nc = _bacc.Bacc("TRN2", target_bir_lowering=False, num_devices=1)
    arrays, args = {}, {}
    for name, value in inputs.items():
        a = _np.ascontiguousarray(value)
        arrays[f"in_{name}"] = a
        args[name] = nc.dram_tensor(f"in_{name}", a.shape, _mybir.dt.from_np(a.dtype), kind="ExternalInput").ap()
    out = nc.dram_tensor("out_rows", (BATCHES, TOKENS, D), F32, kind="ExternalOutput").ap()
    build(nc, args, out)
    r = _run(nc, [arrays], core_ids=[0])
    return r.results[0]["out_rows"]
```
